# Optimizing a Trainium2 kernel written in Bass

```python
import numpy as np
import jax
import jax.numpy as jnp

def _softmax(x, axis=-1):
    return jax.nn.softmax(x, axis=axis)

def _gelu(x):
    return jax.nn.gelu(x, approximate=True)

def _silu(x):
    return jax.nn.silu(x)

def _sigmoid(x):
    return jax.nn.sigmoid(x)

def _layernorm(x, axis=-1, eps=1e-05):
    m = jnp.mean(x, axis=axis, keepdims=True)
    v = jnp.var(x, axis=axis, keepdims=True)
    return (x - m) / jnp.sqrt(v + eps)

def _scatter_add(tgt, idx, src, axis=0):
    return tgt.at[idx].add(src)

def _segment_sum(src, seg, n):
    return jax.ops.segment_sum(src, seg, n)
kernel_name = 'mk_adj_resnorm_d2_adj_r2_ad8b26'

def setup_inputs(seed: int=0):
    np.random.seed(seed)
    _w = jnp.asarray

    def _rec_inputs():
        import jax
        import jax.numpy as jnp
        _gk = jax.random.key(seed)
        x = -9.806e-05 + 1 * jax.random.normal(jax.random.fold_in(_gk, 1), (4096, 64), jnp.float32)
        _a = jax.random.bernoulli(jax.random.fold_in(_gk, 2), 0.000976562, (4096, 4096))
        _a = jnp.logical_or(_a, jnp.swapaxes(_a, -1, -2))
        _a = jnp.logical_or(_a, jnp.eye(4096, dtype=bool))
        adj = _a.astype(jnp.int32)
        return (x, adj)
    x, adj = _rec_inputs()

    def _L0_gnn_setup():
        import jax, jax.numpy as jnp
        import numpy as np
        ALPHA = 0.2
        NEG_BIG = -9000000000000000.0
        key = jax.random.key(seed)
        k1, k2, k3, k4, k5 = jax.random.split(key, 5)
        N, M, F_in, F_out = (4096, 4096, 64, 64)
        item_embs = jax.random.normal(k1, (N, F_in), dtype=jnp.float32)
        entity_embs = jax.random.normal(k2, (M, F_in), dtype=jnp.float32)
        adj = jax.random.randint(k3, (N, M), 0, 2, dtype=jnp.int32)
        W = jax.random.normal(k4, (F_in, F_out), dtype=jnp.float32)
        a = jax.random.normal(k5, (2 * F_out, 1), dtype=jnp.float32)
        return {'item_embs': item_embs, 'entity_embs': entity_embs, 'adj': adj, 'W': W, 'a': a}
    _L0_gnn_all = _L0_gnn_setup()
    _L0_gnn_in = {k: v for k, v in _L0_gnn_all.items() if k in ('entity_embs', 'W', 'a')}
    del _L0_gnn_all

    def _L1_gnn_setup():
        import jax, jax.numpy as jnp
        import numpy as np
        N = 6144
        IN_C = 64
        OUT_C = 64
        NEG_INF = -1000000000.0
        key = jax.random.key(seed)
        k1, k2, k3, k4 = jax.random.split(key, 4)
        x = jax.random.normal(k1, (N, IN_C), dtype=jnp.float32)
        edge_index = jax.random.randint(k2, (N, N), 0, 2, dtype=jnp.int32)
        weight_w = jax.random.normal(k3, (IN_C, OUT_C), dtype=jnp.float32) * (1.0 / np.sqrt(IN_C))
        weight_a = jax.random.normal(k4, (2 * OUT_C, 1), dtype=jnp.float32) * (1.0 / np.sqrt(OUT_C))
        bias = jnp.zeros((OUT_C,), dtype=jnp.float32)
        return {'x': x, 'edge_index': edge_index, 'weight_w': weight_w, 'weight_a': weight_a, 'bias': bias}
    _L1_gnn_all = _L1_gnn_setup()
    _L1_gnn_in = {k: v for k, v in _L1_gnn_all.items() if k in ('weight_w', 'weight_a', 'bias')}
    del _L1_gnn_all
    return {'x': x, 'adj': adj, 'L0_gnn_entity_embs': _L0_gnn_in['entity_embs'], 'L0_gnn_W': _L0_gnn_in['W'], 'L0_gnn_a': _L0_gnn_in['a'], 'L1_gnn_weight_w': _L1_gnn_in['weight_w'], 'L1_gnn_weight_a': _L1_gnn_in['weight_a'], 'L1_gnn_bias': _L1_gnn_in['bias']}

def reference(x, adj, L0_gnn_entity_embs, L0_gnn_W, L0_gnn_a, L1_gnn_weight_w, L1_gnn_weight_a, L1_gnn_bias):
    import jax
    import jax.numpy as jnp

    def _L0_gnn_ref(item_embs, entity_embs, adj, W, a):
        import jax, jax.numpy as jnp
        import numpy as np
        ALPHA = 0.2
        NEG_BIG = -9000000000000000.0
        F_out = W.shape[1]
        Wh = item_embs @ W
        We = entity_embs @ W
        a1 = a[:F_out, 0]
        a2 = a[F_out:, 0]
        scores = (Wh @ a1)[:, None] + (We @ a2)[None, :]
        e = jnp.where(scores > 0, scores, ALPHA * scores)
        e = jnp.where(adj > 0, e, NEG_BIG)
        attention = jax.nn.softmax(e, axis=1)
        entity_emb_weighted = attention @ entity_embs
        h_prime = entity_emb_weighted + item_embs
        return jax.nn.elu(h_prime)

    def _L1_gnn_ref(x, edge_index, weight_w, weight_a, bias):
        import jax, jax.numpy as jnp
        import numpy as np
        N = 6144
        IN_C = 64
        OUT_C = 64
        NEG_INF = -1000000000.0
        wh = x @ weight_w
        a_src = weight_a[:OUT_C, 0]
        a_dst = weight_a[OUT_C:, 0]
        e = (wh @ a_src)[:, None] + (wh @ a_dst)[None, :]
        e = jax.nn.leaky_relu(e, negative_slope=0.01)
        scores = jnp.where(edge_index > 0, e, NEG_INF)
        attention = jax.nn.softmax(scores, axis=1)
        out = attention @ wh
        return out + bias
    x = _layernorm(x + _L0_gnn_ref(x, L0_gnn_entity_embs, adj, L0_gnn_W, L0_gnn_a), axis=-1)
    x = _layernorm(x + _L1_gnn_ref(x, adj, L1_gnn_weight_w, L1_gnn_weight_a, L1_gnn_bias), axis=-1)
    return x

_drawn_inputs = setup_inputs


def setup_inputs(seed=0):
    import zlib

    import numpy as np

    out = dict(_drawn_inputs(seed))
    spreads = {'L1_gnn_bias': (0.0, 0.1)}
    factors = {}
    for name, (base, spread) in spreads.items():
        noise = np.random.default_rng([zlib.crc32(name.encode()), seed]).standard_normal(out[name].shape)
        drawn = base * np.exp(spread * noise) if base else spread * noise
        out[name] = jnp.asarray(drawn.astype(out[name].dtype))
    for name, factor in factors.items():
        out[name] = (out[name] * factor).astype(out[name].dtype)
    return out
```

```python
from contextlib import ExitStack

import concourse.bass as bass
from concourse import mybir

F32 = mybir.dt.float32
BF16 = mybir.dt.bfloat16
FP8 = mybir.dt.float8e4
I8 = mybir.dt.int8
I32 = mybir.dt.int32
ALU = mybir.AluOpType
ACT = mybir.ActivationFunctionType
AX = mybir.AxisListType

P = 128
ALPHAS = (0.2, 0.01)
LN_EPS = 1e-5
PLUS_ONE_AS_INT8 = 56.0
MASK_MARGIN = 60.0


def build(nc, x, adj, E, W0, a0, W1, a1, bias, out):
    N, F = x.shape
    F1 = F + 1
    JT = N // P
    RT = 8
    CW = RT * P
    NC = N // CW
    NCH = 2 * NC
    HALF = N // 2
    HALVES = 2 * RT
    QW = N // NC
    PIECES = NC * RT
    LAG = 2
    PB = 3
    BANK = 512
    LASTS = (NC - 1, NCH - 1)

    u_scr = nc.dram_tensor("u_rows_scratch", [2, N], BF16, kind="Internal").ap()
    s_scr = nc.dram_tensor("S_rows_scratch", [2, N], F32, kind="Internal").ap()

    with ExitStack() as ctx:
        def sb(name, shape, dt=F32):
            return ctx.enter_context(nc.sbuf_tensor(name, shape, dt))

        def sem(name):
            return ctx.enter_context(nc.semaphore(name))

        v = sb("v", [P, JT, N], FP8)
        v_bytes = v[:, :, :].bitcast(I8)
        adj_in = sb("adj_in", [P, 2, HALF], I32)
        u_row = sb("u_row", [P, N], BF16)
        S_row = sb("S_row", [P, 2, CW])
        Pm = sb("Pm", [P, PB, CW])
        VE = sb("VE", [P, JT, F1])
        X = sb("X", [P, JT, F1])
        junk = sb("junk", [P, 2, QW], I8)
        D = sb("D", [P, 2, RT, P], BF16)
        identf = sb("identf", [P, P])
        identb = sb("identb", [P, P], BF16)
        o = sb("o", [P, RT, F1])
        tAB = sb("tAB", [P, RT * (F1 + F)])
        tA = tAB[:, 0:RT * F1].rearrange("p (r f) -> p r f", f=F1)
        tB = tAB[:, RT * F1:].rearrange("p (r f) -> p r f", f=F)
        accs = tAB[0:F1, 0:CW]
        wbc = sb("wbc", [P, 4, F])
        bias_bc = sb("bias_bc", [P, F])
        WE = sb("WE", [F1, 2, F1])
        totW = sb("totW", [P, F1])
        t_col = sb("t_col", [P, JT])
        s_col = sb("s_col", [P, JT])
        S_col = sb("S_col", [P, JT])
        tau_col = sb("tau_col", [P, JT])
        ebias = sb("ebias", [P, JT])
        uS = sb("uS", [P, 2, JT])
        rowsU = sb("rowsU", [JT, P], BF16)
        rowsS = sb("rowsS", [JT, P])
        um = sb("um", [P, RT, NC])
        um8, T8, a8, A8, g8 = (sb(n, [P, RT]) for n in ("um8", "T8", "a8", "A8", "g8"))
        flag = sb("flag", [P, 2, RT])
        rden, tot1, mean, tot2, var, rstd, mhalf = (
            sb(n, [P, RT]) for n in ("rden", "tot1", "mean", "tot2", "var", "rstd", "mhalf"))
        ext = sb("ext", [P, 3])
        g3 = sb("g3", [P, 3])
        uoff = sb("uoff", [P, 2])
        tmin, halfR, Alo1, Alo2, Alo, K = (sb(n, [P, 1]) for n in ("tmin", "halfR", "Alo1", "Alo2", "Alo", "K"))
        tanh_bias = sb("tanh_bias", [P, 1])
        acol = sb("acol", [F, 4])
        onec = sb("onec", [P, 1])

        prod = Pm[:, 0:2, :].rearrange("p a b -> p (a b)").rearrange("p (n f) -> p n f", f=F)
        arep = tB[0:F, :, :].rearrange("p a b -> p (a b)").rearrange("p (k m) -> p k m", m=P)
        wraw = o[0:F, 0:2, 0:F]
        wT = tA[0:F, 0:2, 0:F]
        wabs = tA[:, 2, 0:F]
        colsum = tA[:, 7, :]
        totrep = accs[0:F1, 0:P]

        zps = ctx.enter_context(nc.psum_tensor("zps", [P, 2, CW], F32))
        acc = ctx.enter_context(nc.psum_tensor("acc", [P, 2, CW], F32))

        w_loaded, b_loaded, e_loaded, x_loaded = sem("w_loaded"), sem("b_loaded"), sem("e_loaded"), sem("x_loaded")
        adj_landed = [sem("adj_landed0"), sem("adj_landed1")]
        S_landed = [sem("S_landed0"), sem("S_landed1")]
        u_landed = [sem(f"u_landed{c}") for c in range(NC)]
        scr_written, out_written = sem("scr_written"), sem("out_written")
        memsets, ident_done, identb_done = sem("memsets"), sem("ident_done"), sem("identb_done")
        arep_done, wT_turned, wT_saved = sem("arep_done"), sem("wT_turned"), sem("wT_saved")
        wbc_done, wbc_saved, WE_done = sem("wbc_done"), sem("wbc_saved"), sem("WE_done")
        ext_done, g3_done, ebias_done = sem("ext_done"), sem("g3_done"), sem("ebias_done")
        uS_ready, uS_turned, rows_saved = sem("uS_ready"), sem("uS_turned"), sem("rows_saved")
        colsum_done, tot_done, totrep_saved = sem("colsum_done"), sem("tot_done"), sem("totrep_saved")
        totW_done, totW_saved = sem("totW_done"), sem("totW_saved")
        tanh_done, max_done, D_ready = sem("tanh_done"), sem("max_done"), sem("D_ready")
        turned, z_done, exp_done, pv_done = sem("turned"), sem("z_done"), sem("exp_done"), sem("pv_done")
        acc_saved, proj_done, o_saved = sem("acc_saved"), sem("proj_done"), sem("o_saved")
        flag_added, rden_done, min_done, elu_done = sem("flag_added"), sem("rden_done"), sem("min_done"), sem("elu_done")
        y_done, tot1_done, sq_done, tot2_done = sem("y_done"), sem("tot1_done"), sem("sq_done"), sem("tot2_done")
        rstd_done, new_done = sem("rstd_done"), sem("new_done")
        sprod_done, tprod_done = sem("sprod_done"), sem("tprod_done")
        diag_part = sem("diag_part")
        dve_chain, pool_chain = sem("dve_chain"), sem("pool_chain")

        block = ctx.enter_context(nc.Block())

        def layer(C):
            return C // NC

        def xcols(C):
            return slice(C % NC * RT, C % NC * RT + RT)

        def rows_turned(C):
            return C + 2

        def half_step(m):
            return m * 7 // 4

        def piece_step(n):
            return n * 7 // 8 + 1

        def chain(eng, sem_, count):
            def link(ins):
                count[0] += 1
                ins.then_inc(sem_, 1)
                eng.wait_ge(sem_, count[0])
            return link

        @block.sync
        def _(sp):
            def load_half(H):
                if H >= 2:
                    sp.wait_ge(tanh_done, H - 1)
                sp.dma_start(adj_in[:, H % 2, :], adj[H // 2 * P:(H // 2 + 1) * P, H % 2 * HALF:(H % 2 + 1) * HALF])\
                    .then_inc(adj_landed[H % 2], 16)

            def load_S(C):
                if C >= 2:
                    sp.wait_ge(z_done, JT * (C - 1))
                c = C % NC
                sp.dma_start(S_row[:, C % 2, :], s_scr[layer(C):layer(C) + 1, c * CW:(c + 1) * CW]
                             .broadcast_to([P, CW])).then_inc(S_landed[C % 2], 16)

            def store_rows(l, C, n):
                sp.wait_ge(rows_saved, 2 * (rows_turned(C) if l else 1))
                sl = slice(C * CW, C * CW + n * P)
                sp.dma_start(u_scr[l, sl].rearrange("(n m) -> n m", m=P), rowsU[0:n, :]).then_inc(scr_written, 16)
                sp.dma_start(s_scr[l, sl].rearrange("(n m) -> n m", m=P), rowsS[0:n, :]).then_inc(scr_written, 16)

            def load_u(c):
                sp.dma_start(u_row[:, c * QW:(c + 1) * QW], u_scr[1:2, c * QW:(c + 1) * QW]
                             .broadcast_to([P, QW])).then_inc(u_landed[c], 16)

            def store_out(C):
                c = C % NC
                sp.wait_ge(new_done, C + 1)
                sp.dma_start(out[c * CW:(c + 1) * CW, :].rearrange("(r p) f -> p r f", p=P), tB[:, :, :])\
                    .then_inc(out_written, 16)

            sp.dma_start(VE[:, :, 0:F], E.rearrange("(n p) f -> p n f", p=P)).then_inc(e_loaded, 16)
            sp.dma_start(X[:, :, 0:F], x.rearrange("(n p) f -> p n f", p=P)).then_inc(x_loaded, 16)
            load_half(0)
            load_half(1)
            store_rows(0, 0, JT)
            sp.wait_ge(scr_written, 32)
            sp.dma_start(u_row[:, :], u_scr[0:1, :].broadcast_to([P, N])).then_inc(u_landed[0], 16)
            load_S(0)
            load_S(1)
            for H in range(2, HALVES):
                load_half(H)
            for C in range(NCH):
                if C + 1 < NC:
                    for m in range(HALVES):
                        load_half(HALVES * (C + 1) + m)
                if C == NC - 1:
                    sp.wait_ge(max_done, PIECES * NC)
                    sp.wait_ge(scr_written, 32 * (NC - 1))
                    for c in range(NC - 2):
                        load_u(c)
                    store_rows(1, C - 1, RT)
                    sp.wait_ge(scr_written, 32 * NC)
                    load_u(NC - 2)
                    store_rows(1, C, RT)
                    sp.wait_ge(scr_written, 32 * (NC + 1))
                    load_u(NC - 1)
                    load_S(NC)
                    load_S(NC + 1)
                elif 1 <= C < NC:
                    store_rows(1, C - 1, RT)
                    load_S(C + 1)
                elif NC < C < NCH - 1:
                    load_S(C + 1)
                if C > NC:
                    store_out(C - 1)
            store_out(NCH - 1)
            sp.wait_ge(out_written, 16 * NC)

        def epilogue(eng, ns, link, C, sums=None, squares=None, inverse=None, scores=None):
            b3 = [P, RT, F]
            xs = X[:, xcols(C), 0:F]
            h, tAf, tBf = o[:, :, 0:F], tA[:, :, 0:F], tB[:, :, :]

            def per_row(t):
                return t.unsqueeze(2).broadcast_to(b3)

            def per_feature(t):
                return t.unsqueeze(1).broadcast_to(b3)

            eng.wait_ge(totW_saved, layer(C) + 1)
            eng.wait_ge(proj_done, C + 1)
            eng.wait_ge(D_ready, C + 1)
            link(ns.tensor_tensor(tA[:, :, :], flag[:, C % 2, :].unsqueeze(2).broadcast_to([P, RT, F1]),
                                  totW[:, :].unsqueeze(1).broadcast_to([P, RT, F1]), ALU.mult))
            eng.wait_ge(o_saved, C + 1)
            ns.tensor_tensor(o[:, :, :], o[:, :, :], tA[:, :, :], ALU.add).then_inc(flag_added, 1)
            if C in LASTS:
                reciprocal(C)
            eng.wait_ge(rden_done, C + 1)
            link(ns.tensor_tensor(h, h, per_row(rden[:, :]), ALU.mult))
            if C == 0:
                eng.wait_ge(x_loaded, 16)
            link(ns.tensor_tensor(tBf, h, xs, ALU.add))
            if layer(C) == 0:
                ns.tensor_scalar(tAf, tBf, 0.0, -3.0e38, ALU.min, ALU.max).then_inc(min_done, 1)
                eng.wait_ge(min_done, C + 1)
                link(ns.tensor_tensor(tBf, tBf, tAf, ALU.subtract))
                link(ns.tensor_tensor(tBf, tBf, xs, ALU.add))
                eng.wait_ge(elu_done, C + 1)
                link(ns.tensor_scalar(h, h, 1.0, -1.0, ALU.mult, ALU.add))
                ns.tensor_tensor(tBf, tBf, h, ALU.add).then_inc(y_done, 1)
            else:
                if C == NC:
                    eng.wait_ge(b_loaded, 16)
                ns.tensor_tensor(tBf, tBf, per_feature(bias_bc[:, :]), ALU.add).then_inc(y_done, 1)
            if C in LASTS:
                sums(C)
            eng.wait_ge(tot1_done, C + 1)
            link(ns.tensor_scalar(mean[:, :], tot1[:, :], -1.0 / F, 0.0, ALU.mult, ALU.add))
            link(ns.tensor_tensor(tBf, tBf, per_row(mean[:, :]), ALU.add))
            ns.tensor_tensor(tAf, tBf, tBf, ALU.mult).then_inc(sq_done, 1)
            (squares if C in LASTS else inverse)(C)
            eng.wait_ge(rstd_done, C + 1)
            ns.tensor_tensor(xs if layer(C) == 0 else tBf, tBf, per_row(rstd[:, :]), ALU.mult).then_inc(new_done, 1)
            if layer(C) == 0:
                eng.wait_ge(new_done, C + 1)
                ns.tensor_tensor(tAf, xs, per_feature(wbc[:, 2, :]), ALU.mult).then_inc(sprod_done, 1)
                ns.tensor_tensor(tBf, xs, per_feature(wbc[:, 3, :]), ALU.mult).then_inc(tprod_done, 1)
                if C in LASTS:
                    scores(C)

        def reciprocal(C):
            nc.vector.wait_ge(flag_added, C + 1)
            nc.vector.reciprocal(rden[:, :], o[:, :, F]).then_inc(rden_done, 1)

        @block.gpsimd
        def _(pool):
            link = chain(pool, pool_chain, [0])
            g = nc.gpsimd
            g.memset(identf[:, :], 0.0).then_inc(ident_done, 1)
            g.memset(VE[:, :, F], 1.0).then_inc(memsets, 1)
            g.memset(X[:, :, F], 1.0).then_inc(memsets, 1)
            g.memset(onec[:, :], 1.0).then_inc(memsets, 1)
            g.memset(mhalf[:, :], -0.5).then_inc(memsets, 1)
            pool.wait_ge(ident_done, 1)
            g.affine_select(out=identf[:, :], in_=identf[:, :], compare_op=ALU.not_equal, fill=1.0,
                            base=0, pattern=[[-1, P]], channel_multiplier=1).then_inc(ident_done, 1)

            def inverse(C):
                pool.wait_ge(tot2_done, C + 1)
                link(g.tensor_scalar(var[:, :], tot2[:, :], 1.0 / F, LN_EPS, ALU.mult, ALU.add))
                g.tensor_tensor(rstd[:, :], var[:, :], mhalf[:, :], ALU.pow).then_inc(rstd_done, 1)

            def extremes(l):
                pool.wait_ge(ext_done, l + 1)
                g.partition_all_reduce(g3[:, :], ext[:, :], P, bass.bass_isa.ReduceOp.max).then_inc(g3_done, 1)

            extremes(0)
            pool.wait_ge(memsets, 4)
            pool.wait_ge(wbc_saved, 1)
            for C in range(NCH):
                if C in LASTS:
                    inverse(C)
                else:
                    epilogue(pool, g, link, C, inverse=inverse)
                if C == NC - 1:
                    extremes(1)

        @block.scalar
        def _(act):
            a = nc.scalar
            act.dma_start(wraw[:, 0, :], W0).then_inc(w_loaded, 16)
            act.dma_start(wraw[:, 1, :], W1).then_inc(w_loaded, 16)
            for k in range(4):
                act.dma_start(acol[:, k:k + 1], (a0, a1)[k // 2][k % 2 * F:(k % 2 + 1) * F, :]).then_inc(w_loaded, 16)
            act.dma_start(bias_bc[:, :], bias.rearrange("(one f) -> one f", one=1).broadcast_to([P, F]))\
                .then_inc(b_loaded, 16)
            act.wait_ge(wT_turned, 1)
            a.activation(wT, zps[0:F, :, 0:F], ACT.Copy).then_inc(wT_saved, 1)
            act.wait_ge(wbc_done, 1)
            a.activation(wbc[:, :, :], zps[:, 1, BANK:BANK + 4 * F].rearrange("p (k f) -> p k f", f=F), ACT.Copy)\
                .then_inc(wbc_saved, 1)

            def convert(H):
                act.wait_ge(adj_landed[H % 2], 16 * (H // 2 + 1))
                a.activation(v[:, H // 2, H % 2 * HALF:(H % 2 + 1) * HALF], adj_in[:, H % 2, :], ACT.Tanh,
                             bias=tanh_bias[:, :], scale=40.0, saturate=False).then_inc(tanh_done, 1)

            def save_rows(ps, n, event):
                act.wait_ge(uS_turned, event + 1)
                if event:
                    act.wait_ge(scr_written, 32 * event)
                a.activation(rowsU[0:n, :], ps[0:n, 0:P], ACT.Copy).then_inc(rows_saved, 1)
                a.activation(rowsS[0:n, :], ps[0:n, BANK:BANK + P], ACT.Copy).then_inc(rows_saved, 1)

            def totals(l):
                act.wait_ge(tot_done, l + 1)
                a.activation(totrep, acc[0:F1, 0, 0:1].broadcast_to([F1, P]), ACT.Copy).then_inc(totrep_saved, 1)
                act.wait_ge(totW_done, l + 1)
                if l:
                    act.wait_ge(flag_added, NC)
                a.activation(totW[:, :], acc[:, 0, BANK:BANK + F1], ACT.Copy).then_inc(totW_saved, 1)

            def save_acc(C):
                act.wait_ge(pv_done, JT * (C + 1))
                if 1 <= C <= NC:
                    act.wait_ge(uS_ready, 2 * (C + 1))
                if C > NC:
                    act.wait_ge(out_written, 16 * (C - NC))
                a.activation(accs[:, :], acc[0:F1, C % 2, :], ACT.Copy).then_inc(acc_saved, 1)

            def save_o(C):
                act.wait_ge(proj_done, C + 1)
                if C:
                    act.wait_ge(new_done, C)
                a.activation(o[:, :, :].rearrange("p (b r) f -> p b (r f)", b=2),
                             acc[:, C % 2, :].rearrange("p (b w) -> p b w", b=2)[:, :, 0:RT // 2 * F1], ACT.Copy)\
                    .then_inc(o_saved, 1)

            def elu_exp(C):
                act.wait_ge(min_done, C + 1)
                a.activation(o[:, :, 0:F], tA[:, :, 0:F], ACT.Exp).then_inc(elu_done, 1)

            save_rows(zps[:, 0, :], JT, 0)
            act.wait_ge(identb_done, 2)
            for H in range(4):
                convert(H)
            totals(0)
            for H in range(4, HALVES):
                convert(H)
            for C in range(NCH):
                act.wait_ge(ebias_done, layer(C) + 1)
                for J in range(JT):
                    k = JT * C + J
                    if C % NC:
                        if J == 3:
                            save_acc(C - 1)
                        if J == 5:
                            save_o(C - 1)
                        if J == 10 and layer(C) == 0:
                            elu_exp(C - 1)
                        if J == 23 and layer(C) == 0:
                            save_rows(acc[:, (C - 1) % 2, :], RT, C)
                    if C + 1 < NC:
                        for m in range(HALVES):
                            if half_step(m) == J:
                                convert(HALVES * (C + 1) + m)
                    act.wait_ge(z_done, k + 1)
                    if k >= PB:
                        act.wait_ge(pv_done, k - PB + 1)
                    a.activation(Pm[:, k % PB, :], zps[:, k % 2, :], ACT.Exp, bias=ebias[:, J:J + 1])\
                        .then_inc(exp_done, 1)
                if C in LASTS:
                    save_acc(C)
                    save_o(C)
                    if layer(C) == 0:
                        elu_exp(C)
                        save_rows(acc[:, C % 2, :], RT, NC)
                        totals(1)

        @block.vector
        def _(dve):
            link = chain(dve, dve_chain, [0])
            d = nc.vector
            d.memset(tanh_bias[:, :], -20.0).then_inc(identb_done, 1)
            dve.wait_ge(w_loaded, 96)
            for k in range(4):
                ins = d.tensor_copy(arep[:, k, :], acol[:, k:k + 1].broadcast_to([F, P]))
                ins.then_inc(arep_done, 1)
            dve.wait_ge(ident_done, 2)
            d.tensor_copy(identb[:, :], identf[:, :]).then_inc(identb_done, 1)
            for l in range(2):
                link(d.tensor_copy(WE[:, l, :], identf[0:F1, 0:F1]))
            d.tensor_copy(WE[0:F, 1, 0:F], wraw[:, 1, :]).then_inc(WE_done, 1)

            dve.wait_ge(wbc_saved, 1)
            dve.wait_ge(e_loaded, 16)
            for src, loaded, k, col in ((VE, e_loaded, 1, t_col), (X, x_loaded, 0, s_col)):
                dve.wait_ge(loaded, 16)
                link(d.tensor_tensor(prod, src[:, :, 0:F], wbc[:, k, :].unsqueeze(1).broadcast_to([P, JT, F]), ALU.mult))
                link(d.tensor_reduce(col[:, :], prod, AX.X, ALU.add))

            def scalars(l):
                al = ALPHAS[l]
                link(d.tensor_reduce(ext[:, 0:1], t_col[:, :], AX.X, ALU.max))
                link(d.tensor_reduce(ext[:, 1:2], t_col[:, :], AX.X, ALU.min))
                link(d.tensor_reduce(ext[:, 2:3], s_col[:, :], AX.X, ALU.min))
                d.tensor_scalar(ext[:, 1:3], ext[:, 1:3], -1.0, None, ALU.mult).then_inc(ext_done, 1)
                link(d.tensor_scalar(S_col[:, :], s_col[:, :], -(1.0 - al), None, ALU.mult))
                link(d.tensor_scalar(tau_col[:, :], t_col[:, :], 1.0 - al, None, ALU.mult))
                dve.wait_ge(g3_done, l + 1)
                link(d.tensor_scalar(tmin[:, :], g3[:, 1:2], -1.0, None, ALU.mult))
                if l == 0:
                    link(d.tensor_scalar(uoff[:, 0:1], g3[:, 1:2], 1.0, None, ALU.add))
                link(d.tensor_tensor(halfR[:, :], g3[:, 0:1], g3[:, 1:2], ALU.add))
                link(d.tensor_scalar(halfR[:, :], halfR[:, :], 0.5, MASK_MARGIN, ALU.mult, ALU.add))
                link(d.tensor_scalar(Alo1[:, :], g3[:, 2:3], -(1.0 - al), None, ALU.mult))
                link(d.scalar_tensor_tensor(Alo2[:, :], g3[:, 0:1], -al, Alo1[:, :], ALU.mult, ALU.add))
                link(d.scalar_tensor_tensor(Alo[:, :], g3[:, 0:1], -1.0, Alo2[:, :], ALU.mult, ALU.min))
                link(d.tensor_tensor(K[:, :], Alo[:, :], halfR[:, :], ALU.subtract))
                if l:
                    dve.wait_ge(exp_done, JT * NC)
                d.tensor_scalar(ebias[:, :], t_col[:, :], al, K[:, 0:1], ALU.mult, ALU.add).then_inc(ebias_done, 1)

            def column_totals(l):
                V = (VE, X)[l]
                d.tensor_reduce(colsum, V[:, :, :].rearrange("p n f -> p f n"), AX.X, ALU.add).then_inc(colsum_done, 1)

            def row_max(C, n, r, q):
                at = PIECES * C + n
                if layer(C) == 0:
                    dve.wait_ge(tanh_done, HALVES * C + 2 * r + q // 2 + 1)
                if at >= 2:
                    dve.wait_ge(max_done, at - 1)
                rt = C % NC * RT + r
                d.tensor_tensor_reduce(out=junk[:, at % 2, :], in0=v_bytes[:, rt, q * QW:(q + 1) * QW],
                                       in1=u_row[:, q * QW:(q + 1) * QW], scale=1.0, scalar=-3.0e38,
                                       op0=ALU.mult, op1=ALU.max, accum_out=um[:, r, q:q + 1]).then_inc(max_done, 1)

            def diagonals(C):
                l, xc = layer(C), xcols(C)
                al = ALPHAS[l]
                dve.wait_ge(max_done, PIECES * (C + 1))
                link(d.tensor_reduce(um8[:, :], um[:, :, :], AX.X, ALU.max))
                link(d.tensor_scalar(T8[:, :], um8[:, :], 1.0 / PLUS_ONE_AS_INT8, uoff[:, l:l + 1],
                                     ALU.mult, ALU.subtract))
                link(d.tensor_scalar(T8[:, :], T8[:, :], tmin[:, 0:1], None, ALU.max))
                link(d.scalar_tensor_tensor(a8[:, :], T8[:, :], -al, S_col[:, xc], ALU.mult, ALU.subtract))
                link(d.scalar_tensor_tensor(A8[:, :], T8[:, :], -1.0, a8[:, :], ALU.mult, ALU.min))
                link(d.tensor_scalar(g8[:, :], A8[:, :], K[:, 0:1], None, ALU.subtract))
                if C >= 2:
                    dve.wait_ge(flag_added, C - 1)
                    dve.wait_ge(turned, JT * (C - 1))
                link(d.tensor_scalar(flag[:, C % 2, :], um8[:, :], 0.0, 1.0, ALU.is_lt, ALU.mult))
                for r in range(RT):
                    last = d.tensor_scalar(D[:, C % 2, r, :], identb[:, :], g8[:, r:r + 1], None, ALU.mult)
                    if r < RT - 1:
                        last.then_inc(diag_part, 1)
                    else:
                        dve.wait_ge(diag_part, (RT - 1) * (C + 1))
                        last.then_inc(D_ready, 1)

            def sums(C):
                dve.wait_ge(y_done, C + 1)
                d.tensor_reduce(tot1[:, :], tB[:, :, :], AX.X, ALU.add).then_inc(tot1_done, 1)

            def squares(C):
                dve.wait_ge(sq_done, C + 1)
                d.tensor_reduce(tot2[:, :], tA[:, :, 0:F], AX.X, ALU.add).then_inc(tot2_done, 1)

            def scores(C):
                xc = xcols(C)
                dve.wait_ge(sprod_done, C + 1)
                link(d.tensor_reduce(s_col[:, xc], tA[:, :, 0:F], AX.X, ALU.add))
                dve.wait_ge(tprod_done, C + 1)
                link(d.tensor_reduce(t_col[:, xc], tB[:, :, :], AX.X, ALU.add))
                dve.wait_ge(uS_turned, C + 1)
                d.tensor_scalar(uS[:, 0, 0:RT], t_col[:, xc], uoff[:, 1:2], None, ALU.add).then_inc(uS_ready, 1)
                d.tensor_scalar(uS[:, 1, 0:RT], s_col[:, xc], -(1.0 - ALPHAS[1]), None, ALU.mult)\
                    .then_inc(uS_ready, 1)

            scalars(0)
            d.tensor_scalar(uS[:, 0, :], t_col[:, :], uoff[:, 0:1], None, ALU.add).then_inc(uS_ready, 1)
            d.tensor_copy(uS[:, 1, :], S_col[:, :]).then_inc(uS_ready, 1)
            link(d.scalar_tensor_tensor(wabs, wbc[:, 3, :], -1.0, wbc[:, 3, :], ALU.mult, ALU.max))
            link(d.tensor_reduce(uoff[:, 1:2], wabs, AX.X, ALU.add))
            link(d.tensor_scalar(uoff[:, 1:2], uoff[:, 1:2], float(F) ** 0.5, 1.0, ALU.mult, ALU.add))
            dve.wait_ge(memsets, 2)
            column_totals(0)
            dve.wait_ge(u_landed[0], 16)
            for n in range(PIECES):
                row_max(0, n, n // NC, n % NC)
            diagonals(0)

            for C in range(NCH):
                dve.wait_ge(S_landed[C % 2], 16 * (C // 2 + 1))
                nxt = C + 1
                for J in range(JT):
                    k = JT * C + J
                    if C % NC:
                        if J == 7:
                            reciprocal(C - 1)
                        if J == 13:
                            sums(C - 1)
                        if J == 17:
                            squares(C - 1)
                        if J == 21 and layer(C) == 0:
                            scores(C - 1)
                    dve.wait_ge(turned, k + 1)
                    d.scalar_tensor_tensor(zps[:, k % 2, :], S_row[:, C % 2, :], tau_col[:, J:J + 1],
                                           zps[:, k % 2, :], ALU.max, ALU.add).then_inc(z_done, 1)
                    if nxt == NC:
                        for n in range(PIECES - RT):
                            q, r = n // RT, n % RT
                            if (8 + n if q < NC - 2 else 28 + n % RT // 2) == J:
                                dve.wait_ge(u_landed[q], 16 * (1 + (q == 0)))
                                row_max(NC, n, r, q)
                    elif nxt < NCH:
                        for n in range(PIECES):
                            if piece_step(n) == J:
                                row_max(nxt, n, n // NC, n % NC)
                        if J == JT - 2:
                            diagonals(nxt)
                if C == NC - 1:
                    epilogue(dve, d, link, C, sums, squares, None, scores)
                    scalars(1)
                    dve.wait_ge(new_done, NC)
                    column_totals(1)
                    dve.wait_ge(u_landed[NC - 1], 16)
                    for r in range(RT):
                        row_max(NC, PIECES - RT + r, r, NC - 1)
                    diagonals(NC)
                if C == NCH - 1:
                    epilogue(dve, d, link, C, sums, squares)

        @block.tensor
        def _(pe):
            t = nc.tensor
            pe.wait_ge(w_loaded, 96)
            pe.wait_ge(ident_done, 2)
            for l in range(2):
                last = t.transpose(zps[0:F, l, 0:F], wraw[:, l, :], identf[0:F, 0:F])
            last.then_inc(wT_turned, 1)
            pe.wait_ge(arep_done, 4)
            pe.wait_ge(wT_saved, 1)
            for k in range(4):
                last = t.matmul(zps[:, 1, BANK + k * F:BANK + (k + 1) * F], arep[:, k, :], wT[:, k // 2, :],
                                start=True, stop=True)
            last.then_inc(wbc_done, 1)

            def turn_rows(ps, n, event):
                pe.wait_ge(uS_ready, 2 * (event + 1))
                t.transpose(ps[0:n, 0:P], uS[:, 0, 0:n], identf[:, :])
                t.transpose(ps[0:n, BANK:BANK + P], uS[:, 1, 0:n], identf[:, :]).then_inc(uS_turned, 1)

            def totals(l):
                pe.wait_ge(colsum_done, l + 1)
                t.matmul(acc[0:F1, 0, 0:1], colsum, onec[:, :], start=True, stop=True).then_inc(tot_done, 1)
                pe.wait_ge(totrep_saved, l + 1)
                pe.wait_ge(WE_done, 1)
                t.matmul(acc[:, 0, BANK:BANK + F1], totrep, WE[:, l, :], start=True, stop=True).then_inc(totW_done, 1)

            def project(C):
                pe.wait_ge(acc_saved, C + 1)
                for r in range(RT):
                    at = r // 4 * BANK + r % 4 * F1
                    last = t.matmul(acc[:, C % 2, at:at + F1], accs[:, r * P:(r + 1) * P], WE[:, layer(C), :],
                                    start=True, stop=True)
                last.then_inc(proj_done, 1)

            def product(k):
                C, J = k // JT, k % JT
                if J == 0:
                    pe.wait_ge(totW_saved, layer(C) + 1)
                    if C >= 2:
                        pe.wait_ge(o_saved, C - 1)
                    if 2 <= C <= NC + 1:
                        pe.wait_ge(rows_saved, 2 * rows_turned(C - 2))
                pe.wait_ge(exp_done, k + 1)
                V = (VE, X)[layer(C)]
                for b in range(2):
                    last = t.matmul(acc[0:F1, C % 2, b * BANK:(b + 1) * BANK], V[:, J, :],
                                    Pm[:, k % PB, b * BANK:(b + 1) * BANK], start=(J == 0), stop=(J == JT - 1))
                last.then_inc(pv_done, 1)

            turn_rows(zps[:, 0, :], JT, 0)
            totals(0)
            pe.wait_ge(rows_saved, 2)
            for C in range(NCH):
                pe.wait_ge(D_ready, C + 1)
                for J in range(JT):
                    k = JT * C + J
                    if C % NC:
                        if J == 4:
                            project(C - 1)
                        if J == 22 and layer(C) == 0:
                            pe.wait_ge(o_saved, C)
                            turn_rows(acc[:, (C - 1) % 2, :], RT, C)
                    if k >= 2:
                        pe.wait_ge(exp_done, k - 1)
                    for r in range(RT):
                        last = t.matmul(zps[:, k % 2, r * P:(r + 1) * P],
                                        v[:, C % NC * RT + r, J * P:(J + 1) * P], D[:, C % 2, r, :],
                                        start=True, stop=True)
                    last.then_inc(turned, 1)
                    if k - LAG >= JT * NC * layer(C):
                        product(k - LAG)
                if C in LASTS:
                    for k in range(JT * (C + 1) - LAG, JT * (C + 1)):
                        product(k)
                    project(C)
                    if layer(C) == 0:
                        pe.wait_ge(o_saved, C + 1)
                        turn_rows(acc[:, C % 2, :], RT, NC)
                        totals(1)


_INS = ["x", "adj", "L0_gnn_entity_embs", "L0_gnn_W", "L0_gnn_a", "L1_gnn_weight_w", "L1_gnn_weight_a", "L1_gnn_bias"]


def kernel(**inputs):
    import numpy as _np
    import concourse.bacc as _bacc
    from concourse.bass_utils import run_bass_kernel_spmd as _run

    nc = _bacc.Bacc("TRN2", target_bir_lowering=False, num_devices=1)
    arrays, args = {}, []
    for name in _INS:
        a = _np.ascontiguousarray(inputs[name])
        arrays[f"in_{name}"] = a
        args.append(nc.dram_tensor(f"in_{name}", a.shape, mybir.dt.from_np(a.dtype), kind="ExternalInput").ap())
    out = nc.dram_tensor("out", inputs["x"].shape, F32, kind="ExternalOutput").ap()
    build(nc, *args, out)
    r = _run(nc, [arrays], core_ids=[0])
    return r.results[0]["out"]
```

```python
from contextlib import ExitStack

import concourse.bass as bass
from concourse import mybir

F32 = mybir.dt.float32
BF16 = mybir.dt.bfloat16
FP8 = mybir.dt.float8e4
I8 = mybir.dt.int8
I32 = mybir.dt.int32
ALU = mybir.AluOpType
ACT = mybir.ActivationFunctionType
AX = mybir.AxisListType

P = 128
ALPHAS = (0.2, 0.01)
LN_EPS = 1e-5
PLUS_ONE_AS_INT8 = 56.0
MASK_MARGIN = 60.0
SEEDED = ((5, 11, 17, 23, 29), tuple(range(3, 32, 2)))
WIDTHS = ((4, 8, 8, 8, 4), (2, 6, 8, 8, 6, 2))


def build(nc, x, adj, E, W0, a0, W1, a1, bias, out):
    N, F = x.shape
    F1 = F + 1
    G = 32
    JT = N // P
    chunks = [(l, sum(w[:c]), w[c]) for l, w in enumerate(WIDTHS) for c in range(len(w))]
    NCH = len(chunks)
    NC = len(WIDTHS[0])
    assert all(sum(w) == JT for w in WIDTHS)
    RT = max(max(w) for w in WIDTHS)
    CW = RT * P
    HALF = N // 2
    Q = 4
    QW = N // Q
    AHEAD = 2 * (WIDTHS[0][0] + 2)
    EARLY_Q = 2
    LAG = 2
    SETUP_AT = 8
    PB = 3
    BANK = 512
    FIRSTS = (0, NC)
    LASTS = (NC - 1, NCH - 1)

    u_scr = nc.dram_tensor("u_rows_scratch", [2, N], BF16, kind="Internal").ap()
    s_scr = nc.dram_tensor("S_rows_scratch", [2, N], F32, kind="Internal").ap()

    with ExitStack() as ctx:
        def sb(name, shape, dt=F32):
            return ctx.enter_context(nc.sbuf_tensor(name, shape, dt))

        def sem(name):
            return ctx.enter_context(nc.semaphore(name))

        v = sb("v", [P, JT, N], FP8)
        v_bytes = v[:, :, :].bitcast(I8)
        adj_in = sb("adj_in", [P, 2, HALF], I32)
        u_row = sb("u_row", [P, N], BF16)
        S_row = sb("S_row", [P, 2, CW])
        Pm = sb("Pm", [P, PB, CW])
        VE = sb("VE", [P, JT, F])
        X = sb("X", [P, JT, F])
        junk = sb("junk", [P, 2, QW], I8)
        D = sb("D", [P, 2, RT, P], BF16)
        identf = sb("identf", [P, P])
        identb = sb("identb", [P, P], BF16)
        o = sb("o", [P, RT, F1])
        tAB = sb("tAB", [P, RT * (F1 + F)])
        tA = tAB[:, 0:RT * F1].rearrange("p (r f) -> p r f", f=F1)
        tB = tAB[:, RT * F1:].rearrange("p (r f) -> p r f", f=F)
        acc_sums = tAB[:, 0:CW // 2]
        acc_dens = tAB[:, CW // 2:CW // 2 + 2 * P]
        wbc = sb("wbc", [P, 4, F])
        bias_bc = sb("bias_bc", [P, F])
        W1d = sb("W1d", [P, P])
        pick = sb("pick", [P, 4])
        ones = sb("ones", [P, G])
        totW = sb("totW", [P, F1])
        t_col = sb("t_col", [P, JT])
        s_col = sb("s_col", [P, JT])
        S_col = sb("S_col", [P, JT])
        tau_col = sb("tau_col", [P, JT])
        ntau_col = sb("ntau_col", [P, JT])
        ebias = sb("ebias", [P, 2, JT])
        uS = sb("uS", [P, 2, JT])
        rowsU = sb("rowsU", [JT, P], BF16)
        rowsS = sb("rowsS", [JT, P])
        um = sb("um", [P, RT, Q])
        um8, T8, a8, A8, g8 = (sb(n, [P, RT]) for n in ("um8", "T8", "a8", "A8", "g8"))
        flag = sb("flag", [P, 2, RT])
        rden, tot1, mean, tot2, var, rstd, mhalf = (
            sb(n, [P, RT]) for n in ("rden", "tot1", "mean", "tot2", "var", "rstd", "mhalf"))
        ext = sb("ext", [P, 3])
        g3 = sb("g3", [P, 3])
        uoff = sb("uoff", [P, 2])
        tmin, halfR, Alo1, Alo2, Alo, K = (sb(n, [P, 1]) for n in ("tmin", "halfR", "Alo1", "Alo2", "Alo", "K"))
        tanh_bias = sb("tanh_bias", [P, 1])
        acol = sb("acol", [F, 4])

        prod = Pm[:, 0:2, :].rearrange("p a b -> p (a b)").rearrange("p (n f) -> p n f", f=F)
        arep = tB[0:F, :, :].rearrange("p a b -> p (a b)").rearrange("p (k m) -> p k m", m=P)
        wraw = o[0:F, 0:2, 0:F]
        wT = tA[0:F, 0:2, 0:F]
        wabs = tA[:, 2, 0:F]
        colsum = tA[:, 7, 0:F]
        totrep = tAB[0:F, 0:P]

        zps = ctx.enter_context(nc.psum_tensor("zps", [P, 2, CW], F32))
        acc = ctx.enter_context(nc.psum_tensor("acc", [P, 2, CW], F32))

        w_loaded, b_loaded, e_loaded, x_loaded = sem("w_loaded"), sem("b_loaded"), sem("e_loaded"), sem("x_loaded")
        adj_landed = [sem("adj_landed0"), sem("adj_landed1")]
        S_landed = [sem("S_landed0"), sem("S_landed1")]
        u_landed = [sem(f"u_landed{c}") for c in range(NC)]
        scr_written, out_written = sem("scr_written"), sem("out_written")
        memsets, ident_done, identb_done = sem("memsets"), sem("ident_done"), sem("identb_done")
        arep_done, wT_turned, wT_saved = sem("arep_done"), sem("wT_turned"), sem("wT_saved")
        wbc_done, wbc_saved, pick_done = sem("wbc_done"), sem("wbc_saved"), sem("pick_done")
        W1d_loaded = sem("W1d_loaded")
        ext_done, g3_done, ebias_done = sem("ext_done"), sem("g3_done"), sem("ebias_done")
        uS_ready, uS_turned, rows_saved = sem("uS_ready"), sem("uS_turned"), sem("rows_saved")
        colsum_done, tot_done, totrep_saved = sem("colsum_done"), sem("tot_done"), sem("totrep_saved")
        totW_done, totW_saved = sem("totW_done"), sem("totW_saved")
        tanh_done, max_done, D_ready = sem("tanh_done"), sem("max_done"), sem("D_ready")
        turned, z_done, exp_done, pv_done = sem("turned"), sem("z_done"), sem("exp_done"), sem("pv_done")
        seed_done = sem("seed_done")
        acc_saved, proj_done, o_saved = sem("acc_saved"), sem("proj_done"), sem("o_saved")
        flag_added, rden_done, min_done, elu_done = sem("flag_added"), sem("rden_done"), sem("min_done"), sem("elu_done")
        y_done, tot1_done, sq_done, tot2_done = sem("y_done"), sem("tot1_done"), sem("sq_done"), sem("tot2_done")
        rstd_done, new_done = sem("rstd_done"), sem("new_done")
        sprod_done, tprod_done = sem("sprod_done"), sem("tprod_done")
        dve_chain, pool_chain = sem("dve_chain"), sem("pool_chain")

        block = ctx.enter_context(nc.Block())

        def layer(C):
            return chunks[C][0]

        def R(C):
            return chunks[C][2]

        def xcols(C):
            return slice(chunks[C][1], chunks[C][1] + chunks[C][2])

        def rows(C):
            return slice(chunks[C][1] * P, (chunks[C][1] + chunks[C][2]) * P)

        def seeded(k):
            return k % JT in SEEDED[layer(k // JT)]

        def seeds(k):
            return sum(seeded(i) for i in range(k))

        def group_tiles(C):
            return 2 if R(C) > 4 else 1

        def pieces_before(C):
            return Q * sum(R(c) for c in range(C))

        def stored(C):
            return 16 * (C - NC + 1)

        def halves_at(C, J):
            if C + 1 >= NC:
                return []
            first, end = max(AHEAD, 2 * chunks[C + 1][1]), 2 * (chunks[C + 1][1] + R(C + 1))
            return [h for h in range(first, end) if (h - first) * 27 // (end - first) == J]

        def pieces_at(C, J):
            if C + 1 == NC:
                n = EARLY_Q * R(NC)
                return [(i, i % R(NC), i // R(NC)) for i in range(n) if 20 + i * 12 // n == J]
            if C + 1 == NCH:
                return []
            n = Q * R(C + 1)
            return [(i, i // Q, i % Q) for i in range(n) if i * 28 // n + 1 == J]

        def chain(eng, sem_, count):
            def link(ins):
                count[0] += 1
                ins.then_inc(sem_, 1)
                eng.wait_ge(sem_, count[0])
            return link

        @block.sync
        def _(sp):
            def load_half(H):
                if H >= 2:
                    sp.wait_ge(tanh_done, H - 1)
                sp.dma_start(adj_in[:, H % 2, :], adj[H // 2 * P:(H // 2 + 1) * P, H % 2 * HALF:(H % 2 + 1) * HALF])\
                    .then_inc(adj_landed[H % 2], 16)

            def load_S(C):
                if C >= 2:
                    sp.wait_ge(z_done, JT * (C - 1) - seeds(JT * (C - 1)))
                    sp.wait_ge(seed_done, seeds(JT * (C - 1)))
                sp.dma_start(S_row[:, C % 2, 0:R(C) * P], s_scr[layer(C):layer(C) + 1, rows(C)]
                             .broadcast_to([P, R(C) * P])).then_inc(S_landed[C % 2], 16)

            def store_rows(l, event, sl):
                n = (sl.stop - sl.start) // P
                sp.wait_ge(rows_saved, 2 * (event + 1))
                sp.dma_start(u_scr[l, sl].rearrange("(n m) -> n m", m=P), rowsU[0:n, :]).then_inc(scr_written, 16)
                sp.dma_start(s_scr[l, sl].rearrange("(n m) -> n m", m=P), rowsS[0:n, :]).then_inc(scr_written, 16)

            def load_u(C):
                sp.dma_start(u_row[:, rows(C)], u_scr[1:2, rows(C)].broadcast_to([P, R(C) * P]))\
                    .then_inc(u_landed[C], 16)

            def store_out(C):
                sp.wait_ge(new_done, C + 1)
                sp.dma_start(out[rows(C), :].rearrange("(r p) f -> p r f", p=P), tB[:, 0:R(C), :])\
                    .then_inc(out_written, 16)

            sp.wait_ge(memsets, 1)
            for half in range(2):
                sp.dma_start(W1d[half * F:(half + 1) * F, half * F:(half + 1) * F], W1).then_inc(W1d_loaded, 16)
            sp.dma_start(VE[:, :, :], E.rearrange("(n p) f -> p n f", p=P)).then_inc(e_loaded, 16)
            sp.dma_start(X[:, :, :], x.rearrange("(n p) f -> p n f", p=P)).then_inc(x_loaded, 16)
            for H in range(AHEAD):
                if H == SETUP_AT:
                    store_rows(0, 0, slice(0, N))
                    sp.wait_ge(scr_written, 32)
                    sp.dma_start(u_row[:, :], u_scr[0:1, :].broadcast_to([P, N])).then_inc(u_landed[0], 16)
                    load_S(0)
                    load_S(1)
                load_half(H)
            for C in range(NCH):
                for J in range(JT):
                    for H in halves_at(C, J):
                        load_half(H)
                if C == NC - 1:
                    sp.wait_ge(max_done, pieces_before(NC))
                    sp.wait_ge(scr_written, 32 * (NC - 1))
                    for c in range(NC - 2):
                        load_u(c)
                    store_rows(1, NC - 1, rows(NC - 2))
                    sp.wait_ge(scr_written, 32 * NC)
                    load_u(NC - 2)
                    store_rows(1, NC, rows(NC - 1))
                    sp.wait_ge(scr_written, 32 * (NC + 1))
                    load_u(NC - 1)
                    load_S(NC)
                    load_S(NC + 1)
                elif 1 <= C < NC:
                    store_rows(1, C, rows(C - 1))
                    load_S(C + 1)
                elif NC < C < NCH - 1:
                    load_S(C + 1)
                if C > NC:
                    store_out(C - 1)
            store_out(NCH - 1)
            sp.wait_ge(out_written, stored(NCH - 1))

        def epilogue(eng, ns, link, C, sums=None, squares=None, inverse=None, scores=None):
            n = R(C)
            b3 = [P, n, F]
            xs = X[:, xcols(C), :]
            h, tAf, tBf = o[:, 0:n, 0:F], tA[:, 0:n, 0:F], tB[:, 0:n, :]

            def per_row(t):
                return t.unsqueeze(2).broadcast_to(b3)

            def per_feature(t):
                return t.unsqueeze(1).broadcast_to(b3)

            eng.wait_ge(totW_saved, layer(C) + 1)
            eng.wait_ge(proj_done, C + 1)
            eng.wait_ge(D_ready, C + 1)
            link(ns.tensor_tensor(tA[:, 0:n, :], flag[:, C % 2, 0:n].unsqueeze(2).broadcast_to([P, n, F1]),
                                  totW[:, :].unsqueeze(1).broadcast_to([P, n, F1]), ALU.mult))
            eng.wait_ge(o_saved, C + 1)
            ns.tensor_tensor(o[:, 0:n, :], o[:, 0:n, :], tA[:, 0:n, :], ALU.add).then_inc(flag_added, 1)
            if C in LASTS:
                reciprocal(C)
            eng.wait_ge(rden_done, C + 1)
            link(ns.tensor_tensor(h, h, per_row(rden[:, 0:n]), ALU.mult))
            if C == 0:
                eng.wait_ge(x_loaded, 16)
            link(ns.tensor_tensor(tBf, h, xs, ALU.add))
            if layer(C) == 0:
                ns.tensor_scalar(tAf, tBf, 0.0, -3.0e38, ALU.min, ALU.max).then_inc(min_done, 1)
                eng.wait_ge(min_done, C + 1)
                link(ns.tensor_tensor(tBf, tBf, tAf, ALU.subtract))
                link(ns.tensor_tensor(tBf, tBf, xs, ALU.add))
                eng.wait_ge(elu_done, C + 1)
                link(ns.tensor_scalar(h, h, 1.0, -1.0, ALU.mult, ALU.add))
                ns.tensor_tensor(tBf, tBf, h, ALU.add).then_inc(y_done, 1)
            else:
                if C == NC:
                    eng.wait_ge(b_loaded, 16)
                ns.tensor_tensor(tBf, tBf, per_feature(bias_bc[:, :]), ALU.add).then_inc(y_done, 1)
            if C in LASTS:
                sums(C)
            eng.wait_ge(tot1_done, C + 1)
            link(ns.tensor_scalar(mean[:, 0:n], tot1[:, 0:n], -1.0 / F, 0.0, ALU.mult, ALU.add))
            link(ns.tensor_tensor(tBf, tBf, per_row(mean[:, 0:n]), ALU.add))
            ns.tensor_tensor(tAf, tBf, tBf, ALU.mult).then_inc(sq_done, 1)
            (squares if C in LASTS else inverse)(C)
            eng.wait_ge(rstd_done, C + 1)
            ns.tensor_tensor(xs if layer(C) == 0 else tBf, tBf, per_row(rstd[:, 0:n]), ALU.mult).then_inc(new_done, 1)
            if layer(C) == 0:
                eng.wait_ge(new_done, C + 1)
                ns.tensor_tensor(tAf, xs, per_feature(wbc[:, 2, :]), ALU.mult).then_inc(sprod_done, 1)
                ns.tensor_tensor(tBf, xs, per_feature(wbc[:, 3, :]), ALU.mult).then_inc(tprod_done, 1)
                if C in LASTS:
                    scores(C)

        def reciprocal(C):
            nc.vector.wait_ge(flag_added, C + 1)
            nc.vector.reciprocal(rden[:, 0:R(C)], o[:, 0:R(C), F]).then_inc(rden_done, 1)

        @block.gpsimd
        def _(pool):
            link = chain(pool, pool_chain, [0])
            g = nc.gpsimd
            g.memset(identf[:, :], 0.0).then_inc(ident_done, 1)
            g.memset(W1d[:, :], 0.0).then_inc(memsets, 1)
            g.memset(totW[:, F:F1], float(N)).then_inc(memsets, 1)
            g.memset(ones[:, :], 1.0).then_inc(memsets, 1)
            g.memset(mhalf[:, :], -0.5).then_inc(memsets, 1)
            pool.wait_ge(ident_done, 1)
            g.affine_select(out=identf[:, :], in_=identf[:, :], compare_op=ALU.not_equal, fill=1.0,
                            base=0, pattern=[[-1, P]], channel_multiplier=1).then_inc(ident_done, 1)

            def inverse(C):
                pool.wait_ge(tot2_done, C + 1)
                link(g.tensor_scalar(var[:, 0:R(C)], tot2[:, 0:R(C)], 1.0 / F, LN_EPS, ALU.mult, ALU.add))
                g.tensor_tensor(rstd[:, 0:R(C)], var[:, 0:R(C)], mhalf[:, 0:R(C)], ALU.pow).then_inc(rstd_done, 1)

            def extremes(l):
                pool.wait_ge(ext_done, l + 1)
                g.partition_all_reduce(g3[:, :], ext[:, :], P, bass.bass_isa.ReduceOp.max).then_inc(g3_done, 1)

            extremes(0)
            pool.wait_ge(memsets, 4)
            pool.wait_ge(wbc_saved, 1)
            for C in range(NCH):
                if C in LASTS:
                    inverse(C)
                else:
                    epilogue(pool, g, link, C, inverse=inverse)
                if C == NC - 1:
                    extremes(1)

        @block.scalar
        def _(act):
            a = nc.scalar
            for l, w in enumerate((W0, W1)):
                act.dma_start(wraw[:, l, :], w).then_inc(w_loaded, 16)
            for k in range(4):
                act.dma_start(acol[:, k:k + 1], (a0, a1)[k // 2][k % 2 * F:(k % 2 + 1) * F, :]).then_inc(w_loaded, 16)
            act.dma_start(bias_bc[:, :], bias.rearrange("(one f) -> one f", one=1).broadcast_to([P, F]))\
                .then_inc(b_loaded, 16)
            def convert(H):
                act.wait_ge(adj_landed[H % 2], 16 * (H // 2 + 1))
                a.activation(v[:, H // 2, H % 2 * HALF:(H % 2 + 1) * HALF], adj_in[:, H % 2, :], ACT.Tanh,
                             bias=tanh_bias[:, :], scale=40.0, saturate=False).then_inc(tanh_done, 1)

            def save_rows(ps, n, event):
                act.wait_ge(uS_turned, event + 1)
                if event:
                    act.wait_ge(scr_written, 32 * event)
                a.activation(rowsU[0:n, :], ps[0:n, 0:P], ACT.Copy).then_inc(rows_saved, 1)
                a.activation(rowsS[0:n, :], ps[0:n, BANK:BANK + P], ACT.Copy).then_inc(rows_saved, 1)

            def totals(l):
                act.wait_ge(tot_done, l + 1)
                a.activation(totrep, acc[0:F, 0, 0:1].broadcast_to([F, P]), ACT.Copy).then_inc(totrep_saved, 1)
                act.wait_ge(totW_done, l + 1)
                if l:
                    act.wait_ge(flag_added, NC)
                a.activation(totW[:, 0:F], acc[:, 0, BANK:BANK + F], ACT.Copy).then_inc(totW_saved, 1)

            def save_acc(C):
                act.wait_ge(pv_done, JT * (C + 1))
                if 1 <= C <= NC:
                    act.wait_ge(uS_ready, 2 * (C + 1))
                if C > NC:
                    act.wait_ge(out_written, stored(C - 1))
                w, n = R(C) // 2 * P, group_tiles(C)
                a.activation(acc_sums[:, 0:w], acc[:, C % 2, 0:w], ACT.Copy)
                groups = R(C) // n * G
                a.activation(acc_dens[0:groups, 0:n * P], acc[0:groups, C % 2, BANK:BANK + n * P], ACT.Copy)\
                    .then_inc(acc_saved, 1)

            def save_o(C):
                act.wait_ge(proj_done, C + 1)
                if C:
                    act.wait_ge(new_done, C)
                h, n = R(C) // 2, group_tiles(C)
                groups = R(C) // n
                for s in range(2):
                    a.activation(o[:, s * h:(s + 1) * h, 0:F], acc[:, C % 2, 0:h * P]
                                 .rearrange("p (r s f) -> p s r f", s=2, f=F)[:, s], ACT.Copy)
                a.activation(o[:, 0:R(C), F].rearrange("p (q r) -> p r q", r=n),
                             acc[:, C % 2, BANK:BANK + 4 * n].rearrange("p (r q) -> p r q", q=4)[:, :, 0:groups],
                             ACT.Copy).then_inc(o_saved, 1)

            def elu_exp(C):
                act.wait_ge(min_done, C + 1)
                a.activation(o[:, 0:R(C), 0:F], tA[:, 0:R(C), 0:F], ACT.Exp).then_inc(elu_done, 1)

            act.wait_ge(identb_done, 1)
            for H in range(SETUP_AT):
                convert(H)
            save_rows(zps[:, 0, :], JT, 0)
            for H in range(SETUP_AT, AHEAD):
                if H == SETUP_AT + 1:
                    totals(0)
                convert(H)
            for C in range(NCH):
                act.wait_ge(ebias_done, 3 * (layer(C) + 1))
                act.wait_ge(S_landed[C % 2], 16 * (C // 2 + 1))
                for J in range(JT):
                    k = JT * C + J
                    if C not in FIRSTS:
                        if J == 3:
                            save_acc(C - 1)
                        if J == 5:
                            save_o(C - 1)
                        if J == 10 and layer(C) == 0:
                            elu_exp(C - 1)
                        if J == 23 and layer(C) == 0:
                            save_rows(acc[:, (C - 1) % 2, :], R(C - 1), C)
                    for H in halves_at(C, J):
                        convert(H)
                    if J + 1 < JT and seeded(k + 1):
                        if k >= 1:
                            act.wait_ge(exp_done, k)
                        a.activation(zps[:, (k + 1) % 2, 0:R(C) * P], S_row[:, C % 2, 0:R(C) * P], ACT.Relu,
                                     bias=ntau_col[:, J + 1:J + 2]).then_inc(seed_done, 1)
                    if seeded(k):
                        act.wait_ge(turned, k + 1)
                    else:
                        act.wait_ge(z_done, k + 1 - seeds(k))
                    if k >= PB:
                        act.wait_ge(pv_done, k - PB + 1)
                    a.activation(Pm[:, k % PB, 0:R(C) * P], zps[:, k % 2, 0:R(C) * P], ACT.Exp,
                                 bias=ebias[:, int(seeded(k)), J:J + 1])\
                        .then_inc(exp_done, 1)
                if C in LASTS:
                    save_acc(C)
                    save_o(C)
                    if layer(C) == 0:
                        elu_exp(C)
                        save_rows(acc[:, C % 2, :], R(C), NC)
                        totals(1)

        @block.vector
        def _(dve):
            link = chain(dve, dve_chain, [0])
            d = nc.vector
            d.memset(tanh_bias[:, :], -20.0).then_inc(identb_done, 1)
            dve.wait_ge(w_loaded, 96)
            for k in range(4):
                ins = d.tensor_copy(arep[:, k, :], acol[:, k:k + 1].broadcast_to([F, P]))
                ins.then_inc(arep_done, 1)
            dve.wait_ge(ident_done, 2)
            d.tensor_copy(identb[:, :], identf[:, :]).then_inc(identb_done, 1)
            for q in range(4):
                last = d.tensor_copy(pick[:, q:q + 1], identf[:, q * G:q * G + 1])
            last.then_inc(pick_done, 1)

            dve.wait_ge(wT_turned, 1)
            d.tensor_copy(wT, zps[0:F, :, 0:F]).then_inc(wT_saved, 1)
            dve.wait_ge(wbc_done, 1)
            d.tensor_copy(wbc[:, :, :], zps[:, 1, BANK:BANK + 4 * F].rearrange("p (k f) -> p k f", f=F))\
                .then_inc(wbc_saved, 1)
            dve.wait_ge(wbc_saved, 1)
            dve.wait_ge(e_loaded, 16)
            for src, loaded, k, col in ((VE, e_loaded, 1, t_col), (X, x_loaded, 0, s_col)):
                dve.wait_ge(loaded, 16)
                link(d.tensor_tensor(prod, src[:, :, :], wbc[:, k, :].unsqueeze(1).broadcast_to([P, JT, F]), ALU.mult))
                link(d.tensor_reduce(col[:, :], prod, AX.X, ALU.add))

            def scalars(l):
                al = ALPHAS[l]
                link(d.tensor_reduce(ext[:, 0:1], t_col[:, :], AX.X, ALU.max))
                link(d.tensor_reduce(ext[:, 1:2], t_col[:, :], AX.X, ALU.min))
                link(d.tensor_reduce(ext[:, 2:3], s_col[:, :], AX.X, ALU.min))
                d.tensor_scalar(ext[:, 1:3], ext[:, 1:3], -1.0, None, ALU.mult).then_inc(ext_done, 1)
                link(d.tensor_scalar(S_col[:, :], s_col[:, :], -(1.0 - al), None, ALU.mult))
                link(d.tensor_scalar(tau_col[:, :], t_col[:, :], 1.0 - al, None, ALU.mult))
                dve.wait_ge(g3_done, l + 1)
                link(d.tensor_scalar(tmin[:, :], g3[:, 1:2], -1.0, None, ALU.mult))
                if l == 0:
                    link(d.tensor_scalar(uoff[:, 0:1], g3[:, 1:2], 1.0, None, ALU.add))
                link(d.tensor_tensor(halfR[:, :], g3[:, 0:1], g3[:, 1:2], ALU.add))
                link(d.tensor_scalar(halfR[:, :], halfR[:, :], 0.5, MASK_MARGIN, ALU.mult, ALU.add))
                link(d.tensor_scalar(Alo1[:, :], g3[:, 2:3], -(1.0 - al), None, ALU.mult))
                link(d.scalar_tensor_tensor(Alo2[:, :], g3[:, 0:1], -al, Alo1[:, :], ALU.mult, ALU.add))
                link(d.scalar_tensor_tensor(Alo[:, :], g3[:, 0:1], -1.0, Alo2[:, :], ALU.mult, ALU.min))
                link(d.tensor_tensor(K[:, :], Alo[:, :], halfR[:, :], ALU.subtract))
                if l:
                    dve.wait_ge(exp_done, JT * NC)
                d.tensor_scalar(ntau_col[:, :], t_col[:, :], al - 1.0, None, ALU.mult).then_inc(ebias_done, 1)
                d.tensor_scalar(ebias[:, 0, :], t_col[:, :], al, K[:, 0:1], ALU.mult, ALU.add).then_inc(ebias_done, 1)
                d.tensor_scalar(ebias[:, 1, :], t_col[:, :], K[:, 0:1], None, ALU.add).then_inc(ebias_done, 1)

            def column_totals(l):
                V = (VE, X)[l]
                d.tensor_reduce(colsum, V[:, :, :].rearrange("p n f -> p f n"), AX.X, ALU.add).then_inc(colsum_done, 1)

            def row_max(C, n, r, q):
                at = pieces_before(C) + n
                rt = chunks[C][1] + r
                if layer(C) == 0:
                    dve.wait_ge(tanh_done, 2 * rt + q // 2 + 1)
                if at >= 2:
                    dve.wait_ge(max_done, at - 1)
                d.tensor_tensor_reduce(out=junk[:, at % 2, :], in0=v_bytes[:, rt, q * QW:(q + 1) * QW],
                                       in1=u_row[:, q * QW:(q + 1) * QW], scale=1.0, scalar=-3.0e38,
                                       op0=ALU.mult, op1=ALU.max, accum_out=um[:, r, q:q + 1]).then_inc(max_done, 1)

            def diagonals(C):
                l, xc = layer(C), xcols(C)
                al = ALPHAS[l]
                n = R(C)
                um8_, T_, a_, A_, g_ = (b[:, 0:n] for b in (um8, T8, a8, A8, g8))
                dve.wait_ge(max_done, pieces_before(C + 1))
                link(d.tensor_reduce(um8_, um[:, 0:n, :], AX.X, ALU.max))
                link(d.tensor_scalar(T_, um8_, 1.0 / PLUS_ONE_AS_INT8, uoff[:, l:l + 1], ALU.mult, ALU.subtract))
                link(d.tensor_scalar(T_, T_, tmin[:, 0:1], None, ALU.max))
                link(d.scalar_tensor_tensor(a_, T_, -al, S_col[:, xc], ALU.mult, ALU.subtract))
                link(d.scalar_tensor_tensor(A_, T_, -1.0, a_, ALU.mult, ALU.min))
                link(d.tensor_scalar(g_, A_, K[:, 0:1], None, ALU.subtract))
                if C >= 2:
                    dve.wait_ge(flag_added, C - 1)
                    dve.wait_ge(turned, JT * (C - 1))
                link(d.tensor_scalar(flag[:, C % 2, 0:n], um8_, 0.0, 1.0, ALU.is_lt, ALU.mult))
                for r in range(n):
                    last = d.tensor_scalar(D[:, C % 2, r, :], identb[:, :], g8[:, r:r + 1], None, ALU.mult)
                last.then_inc(D_ready, 1)

            def sums(C):
                dve.wait_ge(y_done, C + 1)
                d.tensor_reduce(tot1[:, 0:R(C)], tB[:, 0:R(C), :], AX.X, ALU.add).then_inc(tot1_done, 1)

            def squares(C):
                dve.wait_ge(sq_done, C + 1)
                d.tensor_reduce(tot2[:, 0:R(C)], tA[:, 0:R(C), 0:F], AX.X, ALU.add).then_inc(tot2_done, 1)

            def scores(C):
                xc = xcols(C)
                dve.wait_ge(sprod_done, C + 1)
                link(d.tensor_reduce(s_col[:, xc], tA[:, 0:R(C), 0:F], AX.X, ALU.add))
                dve.wait_ge(tprod_done, C + 1)
                link(d.tensor_reduce(t_col[:, xc], tB[:, 0:R(C), :], AX.X, ALU.add))
                dve.wait_ge(uS_turned, C + 1)
                d.tensor_scalar(uS[:, 0, 0:R(C)], t_col[:, xc], uoff[:, 1:2], None, ALU.add).then_inc(uS_ready, 1)
                d.tensor_scalar(uS[:, 1, 0:R(C)], s_col[:, xc], -(1.0 - ALPHAS[1]), None, ALU.mult)\
                    .then_inc(uS_ready, 1)

            scalars(0)
            d.tensor_scalar(uS[:, 0, :], t_col[:, :], uoff[:, 0:1], None, ALU.add).then_inc(uS_ready, 1)
            d.tensor_copy(uS[:, 1, :], S_col[:, :]).then_inc(uS_ready, 1)
            link(d.scalar_tensor_tensor(wabs, wbc[:, 3, :], -1.0, wbc[:, 3, :], ALU.mult, ALU.max))
            link(d.tensor_reduce(uoff[:, 1:2], wabs, AX.X, ALU.add))
            link(d.tensor_scalar(uoff[:, 1:2], uoff[:, 1:2], float(F) ** 0.5, 1.0, ALU.mult, ALU.add))
            column_totals(0)
            dve.wait_ge(u_landed[0], 16)
            for n in range(Q * R(0)):
                row_max(0, n, n // Q, n % Q)
            diagonals(0)

            for C in range(NCH):
                dve.wait_ge(S_landed[C % 2], 16 * (C // 2 + 1))
                nxt = C + 1
                for J in range(JT):
                    k = JT * C + J
                    if C not in FIRSTS:
                        if J == 7:
                            reciprocal(C - 1)
                        if J == 13:
                            sums(C - 1)
                        if J == 17:
                            squares(C - 1)
                        if J == 21 and layer(C) == 0:
                            scores(C - 1)
                    if not seeded(k):
                        dve.wait_ge(turned, k + 1)
                        z = zps[:, k % 2, 0:R(C) * P]
                        d.scalar_tensor_tensor(z, S_row[:, C % 2, 0:R(C) * P], tau_col[:, J:J + 1], z,
                                               ALU.max, ALU.add).then_inc(z_done, 1)
                    for n, r, q in pieces_at(C, J):
                        if nxt == NC:
                            for c in range(NC):
                                if q * QW < rows(c).stop and rows(c).start < (q + 1) * QW:
                                    dve.wait_ge(u_landed[c], 16 * (1 + (c == 0)))
                        row_max(nxt, n, r, q)
                    if J == JT - 2 and nxt < NCH and nxt != NC:
                        diagonals(nxt)
                if C == NC - 1:
                    epilogue(dve, d, link, C, sums, squares, None, scores)
                    scalars(1)
                    dve.wait_ge(new_done, NC)
                    column_totals(1)
                    for c in range(NC):
                        dve.wait_ge(u_landed[c], 16 * (1 + (c == 0)))
                    for n in range(EARLY_Q * R(NC), Q * R(NC)):
                        row_max(NC, n, n % R(NC), n // R(NC))
                    diagonals(NC)
                if C == NCH - 1:
                    epilogue(dve, d, link, C, sums, squares)

        @block.tensor
        def _(pe):
            t = nc.tensor
            pe.wait_ge(w_loaded, 96)
            pe.wait_ge(ident_done, 2)
            for l in range(2):
                last = t.transpose(zps[0:F, l, 0:F], wraw[:, l, :], identf[0:F, 0:F])
            last.then_inc(wT_turned, 1)
            pe.wait_ge(arep_done, 4)
            pe.wait_ge(wT_saved, 1)
            for k in range(4):
                last = t.matmul(zps[:, 1, BANK + k * F:BANK + (k + 1) * F], arep[:, k, :], wT[:, k // 2, :],
                                start=True, stop=True)
            last.then_inc(wbc_done, 1)

            def turn_rows(ps, n, event):
                pe.wait_ge(uS_ready, 2 * (event + 1))
                t.transpose(ps[0:n, 0:P], uS[:, 0, 0:n], identf[:, :])
                t.transpose(ps[0:n, BANK:BANK + P], uS[:, 1, 0:n], identf[:, :]).then_inc(uS_turned, 1)

            def totals(l):
                pe.wait_ge(colsum_done, l + 1)
                if l:
                    pe.wait_ge(rows_saved, 2 * (NC + 1))
                t.matmul(acc[0:F, 0, 0:1], colsum, ones[:, 0:1], start=True, stop=True).then_inc(tot_done, 1)
                pe.wait_ge(totrep_saved, l + 1)
                t.matmul(acc[:, 0, BANK:BANK + F], totrep, (identf, W1d)[l][0:F, 0:F], start=True, stop=True)\
                    .then_inc(totW_done, 1)

            def project(C):
                pe.wait_ge(acc_saved, C + 1)
                for r in range(R(C) // 2):
                    t.matmul(acc[:, C % 2, r * P:(r + 1) * P], acc_sums[:, r * P:(r + 1) * P],
                             (identf, W1d)[layer(C)][:, :], start=True, stop=True)
                n, groups = group_tiles(C), R(C) // group_tiles(C)
                for r in range(n):
                    last = t.matmul(acc[:, C % 2, BANK + r * 4:BANK + r * 4 + groups],
                                    acc_dens[0:groups * G, r * P:(r + 1) * P], pick[0:groups * G, 0:groups],
                                    start=True, stop=True)
                last.then_inc(proj_done, 1)

            def product(k):
                C, J = k // JT, k % JT
                if J == 0:
                    pe.wait_ge(totW_saved, layer(C) + 1)
                    if C >= 2:
                        pe.wait_ge(o_saved, C - 1)
                    if 2 <= C <= NC + 1:
                        pe.wait_ge(rows_saved, 2 * C)
                pe.wait_ge(exp_done, k + 1)
                V, w = (VE, X)[layer(C)], R(C) // 2 * P
                first, end = J == 0, J == JT - 1
                for s in range(2):
                    t.matmul(acc[s * F:(s + 1) * F, C % 2, 0:w], V[:, J, :], Pm[:, k % PB, s * w:(s + 1) * w],
                             start=first, stop=end)
                w = group_tiles(C) * P
                for q in range(R(C) * P // w):
                    last = t.matmul(acc[q * G:(q + 1) * G, C % 2, BANK:BANK + w], ones[:, :],
                                    Pm[:, k % PB, q * w:(q + 1) * w], start=first, stop=end)
                last.then_inc(pv_done, 1)

            turn_rows(zps[:, 0, :], JT, 0)
            pe.wait_ge(memsets, 4)
            pe.wait_ge(pick_done, 1)
            pe.wait_ge(W1d_loaded, 32)
            totals(0)
            pe.wait_ge(rows_saved, 2)
            for C in range(NCH):
                pe.wait_ge(D_ready, C + 1)
                for J in range(JT):
                    k = JT * C + J
                    if C not in FIRSTS:
                        if J == 4:
                            project(C - 1)
                        if J == 22 and layer(C) == 0:
                            pe.wait_ge(o_saved, C)
                            turn_rows(acc[:, (C - 1) % 2, :], R(C - 1), C)
                    if k >= 2:
                        pe.wait_ge(exp_done, k - 1)
                    if seeded(k):
                        pe.wait_ge(seed_done, seeds(k) + 1)
                    for r in range(R(C)):
                        last = t.matmul(zps[:, k % 2, r * P:(r + 1) * P],
                                        v[:, chunks[C][1] + r, J * P:(J + 1) * P], D[:, C % 2, r, :],
                                        start=(r * P % BANK == 0 and not seeded(k)), stop=True,
                                        skip_group_check=True)
                    last.then_inc(turned, 1)
                    if k - LAG >= JT * FIRSTS[layer(C)]:
                        product(k - LAG)
                if C in LASTS:
                    for k in range(JT * (C + 1) - LAG, JT * (C + 1)):
                        product(k)
                    project(C)
                    if layer(C) == 0:
                        pe.wait_ge(o_saved, C + 1)
                        turn_rows(acc[:, C % 2, :], R(C), NC)
                        totals(1)


_INS = ["x", "adj", "L0_gnn_entity_embs", "L0_gnn_W", "L0_gnn_a", "L1_gnn_weight_w", "L1_gnn_weight_a", "L1_gnn_bias"]


def kernel(**inputs):
    import numpy as _np
    import concourse.bacc as _bacc
    from concourse.bass_utils import run_bass_kernel_spmd as _run

    nc = _bacc.Bacc("TRN2", target_bir_lowering=False, num_devices=1)
    arrays, args = {}, []
    for name in _INS:
        a = _np.ascontiguousarray(inputs[name])
        arrays[f"in_{name}"] = a
        args.append(nc.dram_tensor(f"in_{name}", a.shape, mybir.dt.from_np(a.dtype), kind="ExternalInput").ap())
    out = nc.dram_tensor("out", inputs["x"].shape, F32, kind="ExternalOutput").ap()
    build(nc, *args, out)
    r = _run(nc, [arrays], core_ids=[0])
    return r.results[0]["out"]
```

```python
from contextlib import ExitStack

import concourse.bass as bass
from concourse import mybir

F32 = mybir.dt.float32
BF16 = mybir.dt.bfloat16
FP8 = mybir.dt.float8e4
I8 = mybir.dt.int8
I32 = mybir.dt.int32
ALU = mybir.AluOpType
ACT = mybir.ActivationFunctionType
AX = mybir.AxisListType

P = 128
ALPHAS = (0.2, 0.01)
LN_EPS = 1e-5
ONE_AS_INT8, HALF_AS_INT8 = 56.0, 48.0
MASK_MARGIN = 60.0
WIDTHS = ((4, 8, 8, 8, 4), (4, 8, 8, 8, 4))
SEEDS = ((22, 28, 28, 22, 4), (28, 20, 16, 8, 0))


def build(nc, x, adj, E, W0, a0, W1, a1, bias, out):
    N, F = x.shape
    F1 = F + 1
    G = 32
    JT = N // P
    chunks = [(l, sum(w[:c]), w[c]) for l, w in enumerate(WIDTHS) for c in range(len(w))]
    NCH = len(chunks)
    NC = len(WIDTHS[0])
    assert all(sum(w) == JT for w in WIDTHS)
    RT = max(max(w) for w in WIDTHS)
    CW = RT * P
    HALF = N // 2
    Q = 4
    QW = N // Q
    BY_ACT = WIDTHS[0][0] + WIDTHS[0][1]
    AHEAD = 2 * (WIDTHS[0][0] + 1)
    EARLY_J = 10
    SEED_AHEAD = 2
    LAG = 2
    SETUP_AT = 3
    GT = 4
    PB = 3
    ZB = 3
    BANK = 512
    FIRSTS = (0, NC)
    LASTS = (NC - 1, NCH - 1)

    u_scr = nc.dram_tensor("u_row_scratch", [N], BF16, kind="Internal").ap()
    s_scr = nc.dram_tensor("S_rows_scratch", [2, N], F32, kind="Internal").ap()

    with ExitStack() as ctx:
        def sb(name, shape, dt=F32):
            return ctx.enter_context(nc.sbuf_tensor(name, shape, dt))

        def sem(name):
            return ctx.enter_context(nc.semaphore(name))

        v = sb("v", [P, JT, N], FP8)
        v_bytes = v[:, :, :].bitcast(I8)
        adj_in = sb("adj_in", [P, 2, HALF], I32)
        u_row = sb("u_row", [P, N], BF16)
        S_row = sb("S_row", [P, 2, CW])
        Pm = sb("Pm", [P, PB, CW])
        VE = sb("VE", [P, JT, F])
        X = sb("X", [P, JT, F])
        junk = sb("junk", [P, 2, 5 * N // 16], I8)
        D = sb("D", [P, 2, RT, P], BF16)
        identf = sb("identf", [P, P])
        identb = sb("identb", [P, P], BF16)
        o = sb("o", [P, RT, F1])
        tAB = sb("tAB", [P, RT * (F1 + F)])
        tA = tAB[:, 0:RT * F1].rearrange("p (r f) -> p r f", f=F1)
        tB = tAB[:, RT * F1:].rearrange("p (r f) -> p r f", f=F)
        acc_sums = tAB[:, 0:CW // 2]
        acc_dens = tAB[:, CW // 2:CW // 2 + 2 * P]
        wbc = sb("wbc", [P, 4, F])
        bias_bc = sb("bias_bc", [P, F])
        W1d = sb("W1d", [P, P])
        pick = sb("pick", [P, 4])
        ones = sb("ones", [P, G])
        onesb = sb("onesb", [P, P], BF16)
        totW = sb("totW", [P, F1])
        t_col = sb("t_col", [P, JT])
        s_col = sb("s_col", [P, JT])
        S_col = sb("S_col", [P, JT])
        tau_col = sb("tau_col", [P, JT])
        ntau_col = sb("ntau_col", [P, JT])
        ebias = sb("ebias", [P, 2, JT])
        uS = sb("uS", [P, 2, JT])
        rowsU = sb("rowsU", [JT, P], BF16)
        rowsS = sb("rowsS", [JT, P])
        um = sb("um", [P, RT, Q])
        um8, T8, a8, A8, g8 = (sb(n, [P, RT]) for n in ("um8", "T8", "a8", "A8", "g8"))
        flag = sb("flag", [P, 2, RT])
        rden, tot1, mean, tot2, var, rstd, mhalf = (
            sb(n, [P, RT]) for n in ("rden", "tot1", "mean", "tot2", "var", "rstd", "mhalf"))
        u_unit = sb("u_unit", [P, JT])
        g_unit = sb("g_unit", [P, JT])
        ext = sb("ext", [P, 3])
        g3 = sb("g3", [P, 3])
        uoff = sb("uoff", [P, 2])
        tmin, halfR, Alo1, Alo2, Alo, K = (sb(n, [P, 1]) for n in ("tmin", "halfR", "Alo1", "Alo2", "Alo", "K"))
        tanh_bias = sb("tanh_bias", [P, 1])
        acol = sb("acol", [F, 4])

        prod = Pm[:, 0:2, :].rearrange("p a b -> p (a b)").rearrange("p (n f) -> p n f", f=F)
        xprod = S_row[:, :, :].rearrange("p a b -> p (a b)").rearrange("p (n f) -> p n f", f=F)
        arep = tB[0:F, :, :].rearrange("p a b -> p (a b)").rearrange("p (k m) -> p k m", m=P)
        wraw = o[0:F, 0:2, 0:F]
        wT = tA[0:F, 0:2, 0:F]
        wabs = tA[:, 2, 0:F]
        colsum = tA[:, 7, 0:F]
        totrep = tAB[0:F, 0:P]

        zps = ctx.enter_context(nc.psum_tensor("zps", [P, ZB, CW], F32))
        acc = ctx.enter_context(nc.psum_tensor("acc", [P, 2, BANK], F32))

        w_loaded, b_loaded, e_loaded, x_loaded = sem("w_loaded"), sem("b_loaded"), sem("e_loaded"), sem("x_loaded")
        adj_landed = [sem("adj_landed0"), sem("adj_landed1")]
        S_landed = [sem("S_landed0"), sem("S_landed1")]
        u_landed = [sem(f"u_landed{c}") for c in range(NC)]
        scr_written, out_written = sem("scr_written"), sem("out_written")
        memsets, ident_done, bias_set = sem("memsets"), sem("ident_done"), sem("bias_set")
        arep_done, wT_turned, wT_saved = sem("arep_done"), sem("wT_turned"), sem("wT_saved")
        wbc_done, wbc_saved, pick_done = sem("wbc_done"), sem("wbc_saved"), sem("pick_done")
        W1d_loaded = sem("W1d_loaded")
        S_first_written = sem("S_first_written")
        S_first_landed = [sem("S_first_landed0"), sem("S_first_landed1")]
        xprod_done, udiag_done, uspread_done, u_saved = (
            sem(n) for n in ("xprod_done", "udiag_done", "uspread_done", "u_saved"))
        ext_done, g3_done, ebias_done = sem("ext_done"), sem("g3_done"), sem("ebias_done")
        uS_ready, uS_turned, rows_saved = sem("uS_ready"), sem("uS_turned"), sem("rows_saved")
        colsum_done, tot_done, totrep_saved = sem("colsum_done"), sem("tot_done"), sem("totrep_saved")
        totW_done, totW_saved = sem("totW_done"), sem("totW_saved")
        tanh_done, compared, max_done, D_ready = sem("tanh_done"), sem("compared"), sem("max_done"), sem("D_ready")
        turned, z_done, exp_done, pv_done = sem("turned"), sem("z_done"), sem("exp_done"), sem("pv_done")
        seed_done = sem("seed_done")
        acc_saved, proj_done, o_saved = sem("acc_saved"), sem("proj_done"), sem("o_saved")
        flag_added, rden_done, min_done, elu_done = sem("flag_added"), sem("rden_done"), sem("min_done"), sem("elu_done")
        y_done, tot1_done, sq_done, tot2_done = sem("y_done"), sem("tot1_done"), sem("sq_done"), sem("tot2_done")
        rstd_done, new_done = sem("rstd_done"), sem("new_done")
        sprod_done, tprod_done = sem("sprod_done"), sem("tprod_done")
        dve_chain, pool_chain = sem("dve_chain"), sem("pool_chain")

        block = ctx.enter_context(nc.Block())

        def layer(C):
            return chunks[C][0]

        def R(C):
            return chunks[C][2]

        def xcols(C):
            return slice(chunks[C][1], chunks[C][1] + chunks[C][2])

        def rows(C):
            return slice(chunks[C][1] * P, (chunks[C][1] + chunks[C][2]) * P)

        def written(event):
            return 32 * min(event, NC - 1) + 16 * (event == NC)

        def early(q):
            n = chunks[NC - 1][1]
            if q == Q - 1:
                return slice(n * P, N)
            return slice(q * n // (Q - 1) * P, (q + 1) * n // (Q - 1) * P)

        def u_of(q):
            return [c for c in range(NC) if early(q).start < rows(c).stop and rows(c).start < early(q).stop]

        users = []
        for C in range(NCH):
            for J in range(JT):
                if C in FIRSTS:
                    users += [("totals", layer(C))] * (J == 2) + [("totals W", layer(C))] * (J == 5)
                else:
                    users += [("sums", C - 1)] * (J == 4) + [("rows", C - 1)] * (J == 22 and layer(C) == 0)
                users += [("step", JT * C + J)]
            if C in LASTS:
                users += [("sums", C)]
                if layer(C) == 0:
                    users += [("u", C), ("rows", C)]
        place = {user: n for n, user in enumerate(users)}

        def buf(what, number):
            return place[what, number] % ZB

        def wait_buf(eng, what, number):
            n = place[what, number]
            if n >= ZB:
                what, number = users[n - ZB]
                eng.wait_ge({"step": exp_done, "sums": o_saved, "rows": rows_saved, "totals": totrep_saved,
                             "totals W": totW_saved, "u": u_saved}[what],
                            {"rows": number + 2, "u": JT // GT + 1}.get(what, number + 1))

        seeded_steps = set()
        for C in range(NCH):
            may = [k for k in range(JT * C, JT * (C + 1)) if place["step", k] >= ZB
                   and users[place["step", k] - ZB][0] == "step" and users[place["step", k] - ZB][1] >= JT * C]
            n = SEEDS[layer(C)][C - FIRSTS[layer(C)]]
            seeded_steps |= {k for i, k in enumerate(may) if (i + 1) * n // len(may) > i * n // len(may)}

        seeds_at = {}
        for k in sorted(seeded_steps):
            seeds_at.setdefault(max(users[place["step", k] - ZB][1] + 1, k - SEED_AHEAD), []).append(k)

        def seeded(k):
            return k in seeded_steps

        def seeds(k):
            return sum(seeded(i) for i in range(k))

        def wait_v(eng, H):
            if H < 2 * BY_ACT:
                eng.wait_ge(tanh_done, H + 1)
            else:
                eng.wait_ge(compared, H + 1 - 2 * BY_ACT)

        def wait_S(eng, C):
            if C < 2:
                eng.wait_ge(S_first_landed[C], 16)
            else:
                eng.wait_ge(S_landed[C % 2], 16 * (C // 2))

        def group_tiles(C):
            return 2 if R(C) > 4 else 1

        def pieces_before(C):
            return Q * sum(R(c) for c in range(C))

        def u_bank(g):
            z = g // 2 % 2 if g < JT // GT else buf("u", NC - 1)
            return zps[:, z, g % 2 * BANK:(g % 2 + 1) * BANK]

        def udiag(g):
            return D[:, g // 2 % 2, g % 2 * GT:(g % 2 + 1) * GT, :]

        def stored(C):
            return 16 * (C - NC + 1)

        def halves_at(C, J):
            if C + 1 >= NC:
                return []
            first, end = max(AHEAD, 2 * chunks[C + 1][1]), 2 * (chunks[C + 1][1] + R(C + 1))
            return [h for h in range(first, end) if (h - first) * 27 // (end - first) == J]

        def pieces_at(C, J):
            if C + 1 == NC:
                n = (Q - 2) * R(NC)
                return [(i, i % R(NC), i // R(NC)) for i in range(n) if EARLY_J + i * (JT - EARLY_J) // n == J]
            if C + 1 == NCH:
                return []
            n = Q * R(C + 1)
            return [(i, i // Q, i % Q) for i in range(n) if i * 29 // n + 1 == J]

        def chain(eng, sem_, count):
            def link(ins):
                count[0] += 1
                ins.then_inc(sem_, 1)
                eng.wait_ge(sem_, count[0])
            return link

        @block.sync
        def _(sp):
            def load_half(H):
                if H >= 2:
                    wait_v(sp, H - 2)
                sp.dma_start(adj_in[:, H % 2, :], adj[H // 2 * P:(H // 2 + 1) * P, H % 2 * HALF:(H % 2 + 1) * HALF])\
                    .then_inc(adj_landed[H % 2], 16)

            def load_S(C):
                if C >= 2:
                    sp.wait_ge(z_done, JT * (C - 1) - seeds(JT * (C - 1)))
                    sp.wait_ge(seed_done, seeds(JT * (C - 1)))
                sp.dma_start(S_row[:, C % 2, 0:R(C) * P], s_scr[layer(C):layer(C) + 1, rows(C)]
                             .broadcast_to([P, R(C) * P])).then_inc(S_landed[C % 2], 16)

            def store_rows(C):
                sp.wait_ge(rows_saved, C + 2)
                if C < NC - 1:
                    sp.dma_start(u_scr[rows(C)].rearrange("(n m) -> n m", m=P), rowsU[0:R(C), :])\
                        .then_inc(scr_written, 16)
                sp.dma_start(s_scr[1, rows(C)].rearrange("(n m) -> n m", m=P), rowsS[0:R(C), :])\
                    .then_inc(scr_written, 16)

            def load_u(C):
                sp.dma_start(u_row[:, rows(C)], u_scr[rows(C)].rearrange("(one n) -> one n", one=1)
                             .broadcast_to([P, R(C) * P])).then_inc(u_landed[C], 16)

            def store_out(C):
                sp.wait_ge(new_done, C + 1)
                sp.dma_start(out[rows(C), :].rearrange("(r p) f -> p r f", p=P), tB[:, 0:R(C), :])\
                    .then_inc(out_written, 16)

            sp.dma_start(wraw[:, 0, :], W0).then_inc(w_loaded, 16)
            for k in range(2):
                sp.dma_start(acol[:, k:k + 1], a0[k * F:(k + 1) * F, :]).then_inc(w_loaded, 16)
            sp.dma_start(VE[:, :, :], E.rearrange("(n p) f -> p n f", p=P)).then_inc(e_loaded, 16)
            for H in range(AHEAD):
                load_half(H)
            for C in range(NCH):
                for J in range(JT):
                    for H in halves_at(C, J):
                        load_half(H)
                if C == NC - 1:
                    sp.wait_ge(max_done, pieces_before(NC))
                    sp.wait_ge(scr_written, written(NC - 2))
                    for c in range(NC - 2):
                        load_u(c)
                    load_S(NC)
                    store_rows(NC - 2)
                    sp.wait_ge(scr_written, written(NC - 1))
                    load_u(NC - 2)
                    store_rows(NC - 1)
                    sp.wait_ge(scr_written, written(NC))
                    load_S(NC + 1)
                elif 1 <= C < NC:
                    store_rows(C - 1)
                    load_S(C + 1)
                elif NC < C < NCH - 1:
                    load_S(C + 1)
                if C > NC:
                    store_out(C - 1)
            store_out(NCH - 1)
            sp.wait_ge(out_written, stored(NCH - 1))

        def epilogue(eng, ns, link, C, sums=None, squares=None, inverse=None, scores=None):
            n = R(C)
            b3 = [P, n, F]
            xs = X[:, xcols(C), :]
            h, tAf, tBf = o[:, 0:n, 0:F], tA[:, 0:n, 0:F], tB[:, 0:n, :]

            def per_row(t):
                return t.unsqueeze(2).broadcast_to(b3)

            def per_feature(t):
                return t.unsqueeze(1).broadcast_to(b3)

            eng.wait_ge(totW_saved, layer(C) + 1)
            eng.wait_ge(proj_done, C + 1)
            eng.wait_ge(D_ready, C + 1)
            link(ns.tensor_tensor(tA[:, 0:n, :], flag[:, C % 2, 0:n].unsqueeze(2).broadcast_to([P, n, F1]),
                                  totW[:, :].unsqueeze(1).broadcast_to([P, n, F1]), ALU.mult))
            eng.wait_ge(o_saved, C + 1)
            ns.tensor_tensor(o[:, 0:n, :], o[:, 0:n, :], tA[:, 0:n, :], ALU.add).then_inc(flag_added, 1)
            if C in LASTS:
                reciprocal(C)
            eng.wait_ge(rden_done, C + 1)
            link(ns.tensor_tensor(h, h, per_row(rden[:, 0:n]), ALU.mult))
            if C == 0:
                eng.wait_ge(x_loaded, 16)
            link(ns.tensor_tensor(tBf, h, xs, ALU.add))
            if layer(C) == 0:
                ns.tensor_scalar(tAf, tBf, 0.0, -3.0e38, ALU.min, ALU.max).then_inc(min_done, 1)
                eng.wait_ge(min_done, C + 1)
                link(ns.tensor_tensor(tBf, tBf, tAf, ALU.subtract))
                link(ns.tensor_tensor(tBf, tBf, xs, ALU.add))
                eng.wait_ge(elu_done, C + 1)
                link(ns.tensor_scalar(h, h, 1.0, -1.0, ALU.mult, ALU.add))
                ns.tensor_tensor(tBf, tBf, h, ALU.add).then_inc(y_done, 1)
            else:
                if C == NC:
                    eng.wait_ge(b_loaded, 16)
                ns.tensor_tensor(tBf, tBf, per_feature(bias_bc[:, :]), ALU.add).then_inc(y_done, 1)
            if C in LASTS:
                sums(C)
            eng.wait_ge(tot1_done, C + 1)
            link(ns.tensor_scalar(mean[:, 0:n], tot1[:, 0:n], -1.0 / F, 0.0, ALU.mult, ALU.add))
            link(ns.tensor_tensor(tBf, tBf, per_row(mean[:, 0:n]), ALU.add))
            ns.tensor_tensor(tAf, tBf, tBf, ALU.mult).then_inc(sq_done, 1)
            (squares if C in LASTS else inverse)(C)
            eng.wait_ge(rstd_done, C + 1)
            ns.tensor_tensor(xs if layer(C) == 0 else tBf, tBf, per_row(rstd[:, 0:n]), ALU.mult).then_inc(new_done, 1)
            if layer(C) == 0:
                eng.wait_ge(new_done, C + 1)
                ns.tensor_tensor(tAf, xs, per_feature(wbc[:, 2, :]), ALU.mult).then_inc(sprod_done, 1)
                ns.tensor_tensor(tBf, xs, per_feature(wbc[:, 3, :]), ALU.mult).then_inc(tprod_done, 1)
                if C in LASTS:
                    scores(C)

        def reciprocal(C):
            nc.vector.wait_ge(flag_added, C + 1)
            nc.vector.reciprocal(rden[:, 0:R(C)], o[:, 0:R(C), F]).then_inc(rden_done, 1)

        @block.gpsimd
        def _(pool):
            link = chain(pool, pool_chain, [0])
            g = nc.gpsimd
            g.memset(identf[:, :], 0.0).then_inc(ident_done, 1)
            g.memset(W1d[:, :], 0.0).then_inc(memsets, 1)
            g.memset(totW[:, F:F1], float(N)).then_inc(memsets, 1)
            g.memset(ones[:, :], 1.0).then_inc(memsets, 1)
            g.memset(onesb[:, :], 1.0).then_inc(memsets, 1)
            for tiles, byte, value in ((slice(0, BY_ACT), ONE_AS_INT8, 1.0), (slice(BY_ACT, JT), HALF_AS_INT8, 0.5)):
                g.memset(u_unit[:, tiles], 1.0 / byte).then_inc(memsets, 1)
                g.memset(g_unit[:, tiles], 1.0 / value).then_inc(memsets, 1)
            g.memset(mhalf[:, :], -0.5).then_inc(memsets, 1)
            pool.wait_ge(ident_done, 1)
            g.affine_select(out=identf[:, :], in_=identf[:, :], compare_op=ALU.not_equal, fill=1.0,
                            base=0, pattern=[[-1, P]], channel_multiplier=1).then_inc(ident_done, 1)

            def inverse(C):
                pool.wait_ge(tot2_done, C + 1)
                link(g.tensor_scalar(var[:, 0:R(C)], tot2[:, 0:R(C)], 1.0 / F, LN_EPS, ALU.mult, ALU.add))
                g.tensor_tensor(rstd[:, 0:R(C)], var[:, 0:R(C)], mhalf[:, 0:R(C)], ALU.pow).then_inc(rstd_done, 1)

            def extremes(l):
                pool.wait_ge(ext_done, l + 1)
                g.partition_all_reduce(g3[:, :], ext[:, :], P, bass.bass_isa.ReduceOp.max).then_inc(g3_done, 1)

            pool.wait_ge(wbc_saved, 1)
            pool.wait_ge(x_loaded, 16)
            g.tensor_tensor(xprod, X[:, :, :], wbc[:, 0, :].unsqueeze(1).broadcast_to([P, JT, F]), ALU.mult)\
                .then_inc(xprod_done, 1)
            extremes(0)
            pool.wait_ge(rows_saved, 1)
            pool.dma_start(s_scr[0, :].rearrange("(n m) -> n m", m=P), rowsS[:, :]).then_inc(S_first_written, 16)
            pool.wait_ge(S_first_written, 16)
            for C in range(2):
                pool.dma_start(S_row[:, C, 0:R(C) * P], s_scr[0:1, rows(C)].broadcast_to([P, R(C) * P]))\
                    .then_inc(S_first_landed[C], 16)
            pool.wait_ge(memsets, 5)
            for C in range(NCH):
                if C in LASTS:
                    inverse(C)
                else:
                    epilogue(pool, g, link, C, inverse=inverse)
                if C == NC - 1:
                    extremes(1)

        @block.scalar
        def _(act):
            a = nc.scalar
            act.dma_start(wraw[:, 1, :], W1).then_inc(w_loaded, 16)
            for k in range(2):
                act.dma_start(acol[:, 2 + k:3 + k], a1[k * F:(k + 1) * F, :]).then_inc(w_loaded, 16)
            act.dma_start(X[:, :, :], x.rearrange("(n p) f -> p n f", p=P)).then_inc(x_loaded, 16)
            act.wait_ge(memsets, 1)
            for half in range(2):
                act.dma_start(W1d[half * F:(half + 1) * F, half * F:(half + 1) * F], W1).then_inc(W1d_loaded, 16)
            act.dma_start(bias_bc[:, :], bias.rearrange("(one f) -> one f", one=1).broadcast_to([P, F]))\
                .then_inc(b_loaded, 16)
            def convert(H):
                act.wait_ge(adj_landed[H % 2], 16 * (H // 2 + 1))
                a.activation(v[:, H // 2, H % 2 * HALF:(H % 2 + 1) * HALF], adj_in[:, H % 2, :], ACT.Tanh,
                             bias=tanh_bias[:, :], scale=40.0, saturate=False).then_inc(tanh_done, 1)

            def save_rows(C):
                act.wait_ge(uS_turned, C + 2)
                if C:
                    act.wait_ge(scr_written, written(C))
                else:
                    act.wait_ge(S_first_written, 16)
                if C < NC - 1:
                    a.activation(rowsU[0:R(C), :], zps[0:R(C), buf("rows", C), 0:P], ACT.Copy)
                a.activation(rowsS[0:R(C), :], zps[0:R(C), buf("rows", C), BANK:BANK + P], ACT.Copy)\
                    .then_inc(rows_saved, 1)

            def save_u(g, sl):
                act.wait_ge(uspread_done, g + 1)
                a.activation(u_row[:, sl], u_bank(g)[:, 0:sl.stop - sl.start], ACT.Copy).then_inc(u_saved, 1)

            def save_totals(l):
                act.wait_ge(tot_done, l + 1)
                a.activation(totrep, zps[0:F, buf("totals", l), 0:1].broadcast_to([F, P]), ACT.Copy)\
                    .then_inc(totrep_saved, 1)

            def save_totals_W(l):
                act.wait_ge(totW_done, l + 1)
                if l:
                    act.wait_ge(flag_added, NC)
                a.activation(totW[:, 0:F], zps[:, buf("totals W", l), 0:F], ACT.Copy)\
                    .then_inc(totW_saved, 1)

            def save_acc(C):
                act.wait_ge(pv_done, JT * (C + 1))
                if 1 <= C <= NC:
                    act.wait_ge(uS_ready, C + 1)
                if C > NC:
                    act.wait_ge(out_written, stored(C - 1))
                w, n = R(C) // 2 * P, group_tiles(C)
                a.activation(acc_sums[:, 0:w], acc[:, 0, 0:w], ACT.Copy)
                groups = R(C) // n * G
                a.activation(acc_dens[0:groups, 0:n * P], acc[0:groups, 1, 0:n * P], ACT.Copy)\
                    .then_inc(acc_saved, 1)

            def save_o(C):
                act.wait_ge(proj_done, C + 1)
                if C:
                    act.wait_ge(new_done, C)
                h, n = R(C) // 2, group_tiles(C)
                groups = R(C) // n
                z = zps[:, buf("sums", C), :]
                for s in range(2):
                    a.activation(o[:, s * h:(s + 1) * h, 0:F], z[:, 0:h * P]
                                 .rearrange("p (r s f) -> p s r f", s=2, f=F)[:, s], ACT.Copy)
                a.activation(o[:, 0:R(C), F].rearrange("p (q r) -> p r q", r=n),
                             z[:, BANK:BANK + 4 * n].rearrange("p (r q) -> p r q", q=4)[:, :, 0:groups],
                             ACT.Copy).then_inc(o_saved, 1)

            def elu_exp(C):
                act.wait_ge(min_done, C + 1)
                a.activation(o[:, 0:R(C), 0:F], tA[:, 0:R(C), 0:F], ACT.Exp).then_inc(elu_done, 1)

            act.wait_ge(bias_set, 1)
            for H in range(SETUP_AT):
                convert(H)
            for g in range(JT // GT):
                save_u(g, slice(g * GT * P, (g + 1) * GT * P))
            for H in range(SETUP_AT, AHEAD):
                convert(H)
            for C in range(NCH):
                act.wait_ge(ebias_done, 3 * (layer(C) + 1))
                wait_S(act, C)
                for J in range(JT):
                    k = JT * C + J
                    if C not in FIRSTS:
                        if J == 2:
                            save_acc(C - 1)
                        if J == 5:
                            save_o(C - 1)
                        if J == 10 and layer(C) == 0:
                            elu_exp(C - 1)
                        if J == 23 and layer(C) == 0:
                            save_rows(C - 1)
                    elif J == 3:
                        save_totals(layer(C))
                    elif J == 6:
                        save_totals_W(layer(C))
                    for H in halves_at(C, J):
                        if H < 2 * BY_ACT:
                            convert(H)
                    for n in seeds_at.get(k, []):
                        wait_buf(act, "step", n)
                        a.activation(zps[:, buf("step", n), 0:R(C) * P], S_row[:, C % 2, 0:R(C) * P], ACT.Relu,
                                     bias=ntau_col[:, n % JT:n % JT + 1]).then_inc(seed_done, 1)
                    if seeded(k):
                        act.wait_ge(turned, k + 1)
                    else:
                        act.wait_ge(z_done, k + 1 - seeds(k))
                    if k >= PB:
                        act.wait_ge(pv_done, k - PB + 1)
                    a.activation(Pm[:, k % PB, 0:R(C) * P], zps[:, buf("step", k), 0:R(C) * P], ACT.Exp,
                                 bias=ebias[:, int(seeded(k)), J:J + 1])\
                        .then_inc(exp_done, 1)
                if C in LASTS:
                    save_acc(C)
                    save_o(C)
                    if layer(C) == 0:
                        elu_exp(C)
                        act.wait_ge(max_done, pieces_before(NC))
                        save_u(JT // GT, rows(C))
                        save_rows(C)

        @block.vector
        def _(dve):
            link = chain(dve, dve_chain, [0])
            d = nc.vector
            d.memset(tanh_bias[:, :], -20.0).then_inc(bias_set, 1)
            dve.wait_ge(w_loaded, 96)
            for k in range(4):
                ins = d.tensor_copy(arep[:, k, :], acol[:, k:k + 1].broadcast_to([F, P]))
                ins.then_inc(arep_done, 1)
            dve.wait_ge(ident_done, 2)
            link(d.tensor_copy(identb[:, :], identf[:, :]))
            for q in range(4):
                last = d.tensor_copy(pick[:, q:q + 1], identf[:, q * G:q * G + 1])
            last.then_inc(pick_done, 1)

            dve.wait_ge(wT_turned, 1)
            d.tensor_copy(wT, zps[0:F, 0:2, 0:F]).then_inc(wT_saved, 1)
            dve.wait_ge(wbc_done, 1)
            d.tensor_copy(wbc[:, :, :], zps[:, 1, BANK:BANK + 4 * F].rearrange("p (k f) -> p k f", f=F))\
                .then_inc(wbc_saved, 1)
            dve.wait_ge(wbc_saved, 1)
            dve.wait_ge(e_loaded, 16)
            link(d.tensor_tensor(prod, VE[:, :, :], wbc[:, 1, :].unsqueeze(1).broadcast_to([P, JT, F]), ALU.mult))
            link(d.tensor_reduce(t_col[:, :], prod, AX.X, ALU.add))
            dve.wait_ge(xprod_done, 1)
            link(d.tensor_reduce(s_col[:, :], xprod, AX.X, ALU.add))

            def scalars(l):
                al = ALPHAS[l]
                link(d.tensor_reduce(ext[:, 0:1], t_col[:, :], AX.X, ALU.max))
                link(d.tensor_reduce(ext[:, 1:2], t_col[:, :], AX.X, ALU.min))
                link(d.tensor_reduce(ext[:, 2:3], s_col[:, :], AX.X, ALU.min))
                d.tensor_scalar(ext[:, 1:3], ext[:, 1:3], -1.0, None, ALU.mult).then_inc(ext_done, 1)
                if l == 0:
                    d.tensor_scalar(uS[:, 1, :], s_col[:, :], -(1.0 - al), None, ALU.mult).then_inc(uS_ready, 1)
                link(d.tensor_scalar(S_col[:, :], s_col[:, :], -(1.0 - al), None, ALU.mult))
                link(d.tensor_scalar(tau_col[:, :], t_col[:, :], 1.0 - al, None, ALU.mult))
                dve.wait_ge(g3_done, l + 1)
                link(d.tensor_scalar(tmin[:, :], g3[:, 1:2], -1.0, None, ALU.mult))
                if l == 0:
                    link(d.tensor_scalar(uoff[:, 0:1], g3[:, 1:2], 1.0, None, ALU.add))
                link(d.tensor_tensor(halfR[:, :], g3[:, 0:1], g3[:, 1:2], ALU.add))
                link(d.tensor_scalar(halfR[:, :], halfR[:, :], 0.5, MASK_MARGIN, ALU.mult, ALU.add))
                link(d.tensor_scalar(Alo1[:, :], g3[:, 2:3], -(1.0 - al), None, ALU.mult))
                link(d.scalar_tensor_tensor(Alo2[:, :], g3[:, 0:1], -al, Alo1[:, :], ALU.mult, ALU.add))
                link(d.scalar_tensor_tensor(Alo[:, :], g3[:, 0:1], -1.0, Alo2[:, :], ALU.mult, ALU.min))
                link(d.tensor_tensor(K[:, :], Alo[:, :], halfR[:, :], ALU.subtract))
                if l:
                    dve.wait_ge(exp_done, JT * NC)
                d.tensor_scalar(ntau_col[:, :], t_col[:, :], al - 1.0, None, ALU.mult).then_inc(ebias_done, 1)
                d.tensor_scalar(ebias[:, 0, :], t_col[:, :], al, K[:, 0:1], ALU.mult, ALU.add).then_inc(ebias_done, 1)
                d.tensor_scalar(ebias[:, 1, :], t_col[:, :], K[:, 0:1], None, ALU.add).then_inc(ebias_done, 1)

            def column_totals(l):
                V = (VE, X)[l]
                d.tensor_reduce(colsum, V[:, :, :].rearrange("p n f -> p f n"), AX.X, ALU.add).then_inc(colsum_done, 1)

            def compare(H):
                dve.wait_ge(adj_landed[H % 2], 16 * (H // 2 + 1))
                d.tensor_scalar(v[:, H // 2, H % 2 * HALF:(H % 2 + 1) * HALF], adj_in[:, H % 2, :], 0.0, 0.5,
                                ALU.is_gt, ALU.subtract, saturate=False).then_inc(compared, 1)

            def row_max(C, n, r, q):
                at = pieces_before(C) + n
                rt = chunks[C][1] + r
                cols = slice(q * QW, (q + 1) * QW)
                if layer(C) == 0:
                    wait_v(dve, 2 * rt + q // 2)
                if C == 0:
                    dve.wait_ge(u_saved, (q + 1) * QW // (GT * P))
                if C == NC:
                    cols = early(q)
                    for c in u_of(q):
                        if c < NC - 1:
                            dve.wait_ge(u_landed[c], 16)
                        else:
                            dve.wait_ge(u_saved, JT // GT + 1)
                if at >= 2:
                    dve.wait_ge(max_done, at - 1)
                d.tensor_tensor_reduce(out=junk[:, at % 2, 0:cols.stop - cols.start],
                                       in0=v_bytes[:, rt, cols], in1=u_row[:, cols], scale=1.0, scalar=-3.0e38,
                                       op0=ALU.mult, op1=ALU.max, accum_out=um[:, r, q:q + 1]).then_inc(max_done, 1)

            def diagonals(C):
                l, xc = layer(C), xcols(C)
                al = ALPHAS[l]
                n = R(C)
                um8_, T_, a_, A_, g_ = (b[:, 0:n] for b in (um8, T8, a8, A8, g8))
                dve.wait_ge(max_done, pieces_before(C + 1))
                link(d.tensor_reduce(um8_, um[:, 0:n, :], AX.X, ALU.max))
                link(d.tensor_tensor(T_, um8_, u_unit[:, xc], ALU.mult))
                link(d.tensor_scalar(T_, T_, uoff[:, l:l + 1], tmin[:, 0:1], ALU.subtract, ALU.max))
                link(d.scalar_tensor_tensor(a_, T_, -al, S_col[:, xc], ALU.mult, ALU.subtract))
                link(d.scalar_tensor_tensor(A_, T_, -1.0, a_, ALU.mult, ALU.min))
                link(d.scalar_tensor_tensor(g_, A_, K[:, 0:1], g_unit[:, xc], ALU.subtract, ALU.mult))
                if C >= 2:
                    dve.wait_ge(flag_added, C - 1)
                    dve.wait_ge(turned, JT * (C - 1))
                link(d.tensor_scalar(flag[:, C % 2, 0:n], um8_, 0.0, 1.0, ALU.is_lt, ALU.mult))
                for r in range(n):
                    last = d.tensor_scalar(D[:, C % 2, r, :], identb[:, :], g8[:, r:r + 1], None, ALU.mult)
                last.then_inc(D_ready, 1)

            def spread_u(g, u, n):
                if g >= GT:
                    dve.wait_ge(uspread_done, g - GT + 1)
                d.tensor_tensor(udiag(g)[:, 0:n, :], identb[:, :].unsqueeze(1).broadcast_to([P, n, P]),
                                u.unsqueeze(2).broadcast_to([P, n, P]), ALU.mult).then_inc(udiag_done, 1)

            def sums(C):
                dve.wait_ge(y_done, C + 1)
                d.tensor_reduce(tot1[:, 0:R(C)], tB[:, 0:R(C), :], AX.X, ALU.add).then_inc(tot1_done, 1)

            def squares(C):
                dve.wait_ge(sq_done, C + 1)
                d.tensor_reduce(tot2[:, 0:R(C)], tA[:, 0:R(C), 0:F], AX.X, ALU.add).then_inc(tot2_done, 1)

            def scores(C):
                xc = xcols(C)
                dve.wait_ge(sprod_done, C + 1)
                link(d.tensor_reduce(s_col[:, xc], tA[:, 0:R(C), 0:F], AX.X, ALU.add))
                dve.wait_ge(tprod_done, C + 1)
                link(d.tensor_reduce(t_col[:, xc], tB[:, 0:R(C), :], AX.X, ALU.add))
                dve.wait_ge(uS_turned, C + 1)
                d.tensor_scalar(uS[:, 0, 0:R(C)], t_col[:, xc], uoff[:, 1:2], None, ALU.add)
                d.tensor_scalar(uS[:, 1, 0:R(C)], s_col[:, xc], -(1.0 - ALPHAS[1]), None, ALU.mult)\
                    .then_inc(uS_ready, 1)

            scalars(0)
            link(d.tensor_scalar(uS[:, 0, :], t_col[:, :], uoff[:, 0:1], None, ALU.add))
            for g in range(JT // GT):
                spread_u(g, uS[:, 0, g * GT:(g + 1) * GT], GT)
            dve.wait_ge(uS_turned, 1)
            d.tensor_copy(rowsS[:, :], acc[0:JT, 1, 0:P]).then_inc(rows_saved, 1)
            link(d.scalar_tensor_tensor(wabs, wbc[:, 3, :], -1.0, wbc[:, 3, :], ALU.mult, ALU.max))
            link(d.tensor_reduce(uoff[:, 1:2], wabs, AX.X, ALU.add))
            link(d.tensor_scalar(uoff[:, 1:2], uoff[:, 1:2], float(F) ** 0.5, 1.0, ALU.mult, ALU.add))
            dve.wait_ge(memsets, 9)
            for n in range(Q * R(0)):
                row_max(0, n, n // Q, n % Q)
            diagonals(0)

            for C in range(NCH):
                wait_S(dve, C)
                nxt = C + 1
                for J in range(JT):
                    k = JT * C + J
                    if C not in FIRSTS:
                        if J == 7:
                            reciprocal(C - 1)
                        if J == 13:
                            sums(C - 1)
                        if J == 17:
                            squares(C - 1)
                        if J == 21 and layer(C) == 0:
                            scores(C - 1)
                    if not seeded(k):
                        dve.wait_ge(turned, k + 1)
                        z = zps[:, buf("step", k), 0:R(C) * P]
                        d.scalar_tensor_tensor(z, S_row[:, C % 2, 0:R(C) * P], tau_col[:, J:J + 1], z,
                                               ALU.max, ALU.add).then_inc(z_done, 1)
                    if J == 1 and C in FIRSTS:
                        column_totals(layer(C))
                    for H in halves_at(C, J):
                        if H >= 2 * BY_ACT:
                            compare(H)
                    for n, r, q in pieces_at(C, J):
                        row_max(nxt, n, r, q)
                    if J == JT - 2 and nxt < NCH and nxt != NC:
                        diagonals(nxt)
                if C == NC - 1:
                    for n in range((Q - 2) * R(NC), (Q - 1) * R(NC)):
                        row_max(NC, n, n % R(NC), n // R(NC))
                    epilogue(dve, d, link, C, sums, squares, None, scores)
                    dve.wait_ge(uS_ready, NC + 1)
                    spread_u(JT // GT, uS[:, 0, 0:R(C)], R(C))
                    scalars(1)
                    for n in range((Q - 1) * R(NC), Q * R(NC)):
                        row_max(NC, n, n % R(NC), n // R(NC))
                    diagonals(NC)
                if C == NCH - 1:
                    epilogue(dve, d, link, C, sums, squares)

        @block.tensor
        def _(pe):
            t = nc.tensor
            pe.wait_ge(w_loaded, 96)
            pe.wait_ge(ident_done, 2)
            for l in range(2):
                last = t.transpose(zps[0:F, l, 0:F], wraw[:, l, :], identf[0:F, 0:F])
            last.then_inc(wT_turned, 1)
            pe.wait_ge(arep_done, 4)
            pe.wait_ge(wT_saved, 1)
            for k in range(4):
                last = t.matmul(zps[:, 1, BANK + k * F:BANK + (k + 1) * F], arep[:, k, :], wT[:, k // 2, :],
                                start=True, stop=True)
            last.then_inc(wbc_done, 1)

            def turn_rows(C):
                pe.wait_ge(uS_ready, C + 2)
                wait_buf(pe, "rows", C)
                z, n = buf("rows", C), R(C)
                if C < NC - 1:
                    t.transpose(zps[0:n, z, 0:P], uS[:, 0, 0:n], identf[:, :])
                t.transpose(zps[0:n, z, BANK:BANK + P], uS[:, 1, 0:n], identf[:, :]).then_inc(uS_turned, 1)

            def spread_u(g, n):
                pe.wait_ge(udiag_done, g + 1)
                if g == JT // GT:
                    wait_buf(pe, "u", NC - 1)
                elif g >= GT:
                    pe.wait_ge(u_saved, g - GT + 1)
                t.matmul(u_bank(g)[:, 0:n * P], onesb[:, :], udiag(g)[:, 0:n, :].rearrange("p n m -> p (n m)"),
                         start=True, stop=True).then_inc(uspread_done, 1)

            def totals(l):
                pe.wait_ge(colsum_done, l + 1)
                wait_buf(pe, "totals", l)
                t.matmul(zps[0:F, buf("totals", l), 0:1], colsum, ones[:, 0:1], start=True, stop=True)\
                    .then_inc(tot_done, 1)

            def totals_W(l):
                pe.wait_ge(totrep_saved, l + 1)
                wait_buf(pe, "totals W", l)
                t.matmul(zps[:, buf("totals W", l), 0:F], totrep, (identf, W1d)[l][0:F, 0:F],
                         start=True, stop=True).then_inc(totW_done, 1)

            def project(C):
                pe.wait_ge(acc_saved, C + 1)
                wait_buf(pe, "sums", C)
                z = buf("sums", C)
                for r in range(R(C) // 2):
                    t.matmul(zps[:, z, r * P:(r + 1) * P], acc_sums[:, r * P:(r + 1) * P],
                             (identf, W1d)[layer(C)][:, :], start=True, stop=True)
                n, groups = group_tiles(C), R(C) // group_tiles(C)
                for r in range(n):
                    last = t.matmul(zps[:, z, BANK + r * 4:BANK + r * 4 + groups],
                                    acc_dens[0:groups * G, r * P:(r + 1) * P], pick[0:groups * G, 0:groups],
                                    start=True, stop=True)
                last.then_inc(proj_done, 1)

            def product(k):
                C, J = k // JT, k % JT
                if J == 0:
                    if C == 0:
                        pe.wait_ge(rows_saved, 1)
                    else:
                        pe.wait_ge(acc_saved, C)
                pe.wait_ge(exp_done, k + 1)
                V, w = (VE, X)[layer(C)], R(C) // 2 * P
                first, end = J == 0, J == JT - 1
                for s in range(2):
                    t.matmul(acc[s * F:(s + 1) * F, 0, 0:w], V[:, J, :], Pm[:, k % PB, s * w:(s + 1) * w],
                             start=first, stop=end)
                w = group_tiles(C) * P
                for q in range(R(C) * P // w):
                    last = t.matmul(acc[q * G:(q + 1) * G, 1, 0:w], ones[:, :],
                                    Pm[:, k % PB, q * w:(q + 1) * w], start=first, stop=end)
                last.then_inc(pv_done, 1)

            pe.wait_ge(uS_ready, 1)
            t.transpose(acc[0:JT, 1, 0:P], uS[:, 1, 0:JT], identf[:, :]).then_inc(uS_turned, 1)
            pe.wait_ge(memsets, 5)
            pe.wait_ge(pick_done, 1)
            pe.wait_ge(W1d_loaded, 32)
            pe.wait_ge(wbc_saved, 1)
            for g in range(JT // GT):
                spread_u(g, GT)
            pe.wait_ge(u_saved, JT // GT)
            for C in range(NCH):
                pe.wait_ge(D_ready, C + 1)
                for J in range(JT):
                    k = JT * C + J
                    if C not in FIRSTS:
                        if J == 4:
                            project(C - 1)
                        if J == 22 and layer(C) == 0:
                            turn_rows(C - 1)
                    elif J == 2:
                        totals(layer(C))
                    elif J == 5:
                        totals_W(layer(C))
                    if seeded(k):
                        pe.wait_ge(seed_done, seeds(k) + 1)
                    else:
                        wait_buf(pe, "step", k)
                    for r in range(R(C)):
                        last = t.matmul(zps[:, buf("step", k), r * P:(r + 1) * P],
                                        v[:, chunks[C][1] + r, J * P:(J + 1) * P], D[:, C % 2, r, :],
                                        start=(r * P % BANK == 0 and not seeded(k)), stop=True,
                                        skip_group_check=True)
                    last.then_inc(turned, 1)
                    if k - LAG >= JT * FIRSTS[layer(C)]:
                        product(k - LAG)
                if C in LASTS:
                    for k in range(JT * (C + 1) - LAG, JT * (C + 1)):
                        product(k)
                    project(C)
                    if layer(C) == 0:
                        spread_u(JT // GT, R(C))
                        turn_rows(C)


_INS = ["x", "adj", "L0_gnn_entity_embs", "L0_gnn_W", "L0_gnn_a", "L1_gnn_weight_w", "L1_gnn_weight_a", "L1_gnn_bias"]


def kernel(**inputs):
    import numpy as _np
    import concourse.bacc as _bacc
    from concourse.bass_utils import run_bass_kernel_spmd as _run

    nc = _bacc.Bacc("TRN2", target_bir_lowering=False, num_devices=1)
    arrays, args = {}, []
    for name in _INS:
        a = _np.ascontiguousarray(inputs[name])
        arrays[f"in_{name}"] = a
        args.append(nc.dram_tensor(f"in_{name}", a.shape, mybir.dt.from_np(a.dtype), kind="ExternalInput").ap())
    out = nc.dram_tensor("out", inputs["x"].shape, F32, kind="ExternalOutput").ap()
    build(nc, *args, out)
    r = _run(nc, [arrays], core_ids=[0])
    return r.results[0]["out"]
```
